# Optimizing a Trainium2 kernel written in Bass

```python
import numpy as np
import jax
import jax.numpy as jnp

def _softmax(x, axis=-1):
    return jax.nn.softmax(x, axis=axis)

def _gelu(x):
    return jax.nn.gelu(x, approximate=True)

def _silu(x):
    return jax.nn.silu(x)

def _sigmoid(x):
    return jax.nn.sigmoid(x)

def _layernorm(x, axis=-1, eps=1e-05):
    m = jnp.mean(x, axis=axis, keepdims=True)
    v = jnp.var(x, axis=axis, keepdims=True)
    return (x - m) / jnp.sqrt(v + eps)

def _scatter_add(tgt, idx, src, axis=0):
    return tgt.at[idx].add(src)

def _segment_sum(src, seg, n):
    return jax.ops.segment_sum(src, seg, n)
kernel_name = 'mk_adj_resnorm_d2_adj_r2_00f670'

def setup_inputs(seed: int=0):
    np.random.seed(seed)
    _w = jnp.asarray

    def _rec_inputs():
        import jax
        import jax.numpy as jnp
        _gk = jax.random.key(seed)
        x = -0.0004039 + 1 * jax.random.normal(jax.random.fold_in(_gk, 1), (16, 512, 384), jnp.float32)
        _a = jax.random.bernoulli(jax.random.fold_in(_gk, 2), 0.0078125, (16, 512, 512))
        _a = jnp.logical_or(_a, jnp.swapaxes(_a, -1, -2))
        _a = jnp.logical_or(_a, jnp.eye(512, dtype=bool))
        _af = _a.astype(jnp.float32)
        adj = _af
        return (x, adj)
    x, adj = _rec_inputs()

    def _L0_gnn_setup():
        import jax, jax.numpy as jnp
        import numpy as np
        B, S, H, L = (32, 256, 384, 2)

        def _layer_norm(z, a, b, eps=0.001):
            mu = jnp.mean(z, axis=-1, keepdims=True)
            sigma = jnp.std(z, axis=-1, keepdims=True, ddof=1)
            return (z - mu) / (sigma + eps) * a + b
        key = jax.random.key(seed)
        ks = jax.random.split(key, 6)
        hidden_state = jax.random.normal(ks[0], (B, S, H), dtype=jnp.float32)
        adjacency_matrix = (jax.random.uniform(ks[1], (B, S, S)) < 0.2).astype(jnp.float32)
        W_left = 0.05 * jax.random.normal(ks[2], (L, H, H), dtype=jnp.float32)
        W_right = 0.05 * jax.random.normal(ks[3], (L, H, H), dtype=jnp.float32)
        W_lin = 0.05 * jax.random.normal(ks[4], (L, H, H), dtype=jnp.float32)
        b_lin = jnp.zeros((L, H), dtype=jnp.float32)
        ln_a = jnp.ones((L, H), dtype=jnp.float32)
        ln_b = jnp.zeros((L, H), dtype=jnp.float32)
        return {'hidden_state': hidden_state, 'adjacency_matrix': adjacency_matrix, 'W_left': W_left, 'W_right': W_right, 'W_lin': W_lin, 'b_lin': b_lin, 'ln_a': ln_a, 'ln_b': ln_b}
    _L0_gnn_all = _L0_gnn_setup()
    _L0_gnn_in = {k: v for k, v in _L0_gnn_all.items() if k in ('W_left', 'W_right', 'W_lin', 'b_lin', 'ln_a', 'ln_b')}
    del _L0_gnn_all

    def _L1_gnn_setup():
        import jax, jax.numpy as jnp
        import numpy as np
        B, N, D, H = (8, 512, 384, 12)
        HD = D // H

        def _split_heads(x):
            b, n, _ = x.shape
            return x.reshape(b, n, H, HD).transpose(0, 2, 1, 3)
        key = jax.random.key(seed)
        ks = jax.random.split(key, 10)
        input_graph = jax.random.normal(ks[0], (B, N, D), dtype=jnp.float32)
        u = jax.random.uniform(ks[1], (B, N, N), dtype=jnp.float32)
        keep = jax.random.uniform(ks[2], (B, N, N)) < 0.15
        adj = jnp.where(keep, u, 0.0)
        s = 1.0 / np.sqrt(D)
        Wq = jax.random.normal(ks[3], (D, D), dtype=jnp.float32) * s
        bq = jnp.zeros((D,), dtype=jnp.float32)
        Wk = jax.random.normal(ks[4], (D, D), dtype=jnp.float32) * s
        bk = jnp.zeros((D,), dtype=jnp.float32)
        Wv = jax.random.normal(ks[5], (D, D), dtype=jnp.float32) * s
        bv = jnp.zeros((D,), dtype=jnp.float32)
        beta = jnp.asarray(0.1, dtype=jnp.float32)
        return {'input_graph': input_graph, 'adj': adj, 'Wq': Wq, 'bq': bq, 'Wk': Wk, 'bk': bk, 'Wv': Wv, 'bv': bv, 'beta': beta}
    _L1_gnn_all = _L1_gnn_setup()
    _L1_gnn_in = {k: v for k, v in _L1_gnn_all.items() if k in ('Wq', 'bq', 'Wk', 'bk', 'Wv', 'bv', 'beta')}
    del _L1_gnn_all
    return {'x': x, 'adj': adj, 'L0_gnn_W_left': _L0_gnn_in['W_left'], 'L0_gnn_W_right': _L0_gnn_in['W_right'], 'L0_gnn_W_lin': _L0_gnn_in['W_lin'], 'L0_gnn_b_lin': _L0_gnn_in['b_lin'], 'L0_gnn_ln_a': _L0_gnn_in['ln_a'], 'L0_gnn_ln_b': _L0_gnn_in['ln_b'], 'L1_gnn_Wq': _L1_gnn_in['Wq'], 'L1_gnn_bq': _L1_gnn_in['bq'], 'L1_gnn_Wk': _L1_gnn_in['Wk'], 'L1_gnn_bk': _L1_gnn_in['bk'], 'L1_gnn_Wv': _L1_gnn_in['Wv'], 'L1_gnn_bv': _L1_gnn_in['bv'], 'L1_gnn_beta': _L1_gnn_in['beta']}

def reference(x, adj, L0_gnn_W_left, L0_gnn_W_right, L0_gnn_W_lin, L0_gnn_b_lin, L0_gnn_ln_a, L0_gnn_ln_b, L1_gnn_Wq, L1_gnn_bq, L1_gnn_Wk, L1_gnn_bk, L1_gnn_Wv, L1_gnn_bv, L1_gnn_beta):
    import jax
    import jax.numpy as jnp

    def _L0_gnn_ref(hidden_state, adjacency_matrix, W_left, W_right, W_lin, b_lin, ln_a, ln_b):
        import jax, jax.numpy as jnp
        import numpy as np
        B, S, H, L = (32, 256, 384, 2)

        def _layer_norm(z, a, b, eps=0.001):
            mu = jnp.mean(z, axis=-1, keepdims=True)
            sigma = jnp.std(z, axis=-1, keepdims=True, ddof=1)
            return (z - mu) / (sigma + eps) * a + b
        temper = float(np.sqrt(H))
        adj = adjacency_matrix
        adj_tri = jnp.triu(adj, k=1)
        diag_mask = jnp.triu(adj, k=0) - adj_tri
        h = hidden_state
        for l in range(L):
            m_left = jnp.einsum('bsh,oh->bso', h, W_left[l])
            m_right = jnp.einsum('bsh,oh->bso', h, W_right[l])
            u_left = jnp.einsum('bih,bjh->bij', h, m_left) / temper
            u_right = jnp.einsum('bih,bjh->bij', h, m_right) / temper
            u = u_left * adj_tri + u_left * diag_mask + u_right * jnp.swapaxes(adj_tri, 1, 2)
            delta_exp_u = jnp.exp(u) * adj
            attention = delta_exp_u / (jnp.sum(delta_exp_u, axis=2, keepdims=True) + 1e-10)
            h_lin = jnp.einsum('bsh,oh->bso', h, W_lin[l]) + b_lin[l]
            ctx = jnp.matmul(attention, h_lin)
            h = jax.nn.relu(_layer_norm(ctx, ln_a[l], ln_b[l]))
        return h

    def _L1_gnn_ref(input_graph, adj, Wq, bq, Wk, bk, Wv, bv, beta):
        import jax, jax.numpy as jnp
        import numpy as np
        B, N, D, H = (8, 512, 384, 12)
        HD = D // H

        def _split_heads(x):
            b, n, _ = x.shape
            return x.reshape(b, n, H, HD).transpose(0, 2, 1, 3)
        q = _split_heads(input_graph @ Wq + bq)
        k = _split_heads(input_graph @ Wk + bk)
        v = _split_heads(input_graph @ Wv + bv)
        scores = jnp.einsum('bhqd,bhkd->bhqk', q, k) / jnp.sqrt(jnp.asarray(HD, input_graph.dtype))
        adj_e = adj[:, None, :, :]
        scores = scores + beta * adj_e
        scores = jnp.where(adj_e > 0, scores, jnp.asarray(-9000000000000000.0, scores.dtype))
        probs = jax.nn.softmax(scores, axis=-1)
        out = jnp.einsum('bhqk,bhkd->bhqd', probs, v)
        return out.transpose(0, 2, 1, 3).reshape(input_graph.shape[0], input_graph.shape[1], D)
    x = _layernorm(x + _L0_gnn_ref(x, adj, L0_gnn_W_left, L0_gnn_W_right, L0_gnn_W_lin, L0_gnn_b_lin, L0_gnn_ln_a, L0_gnn_ln_b), axis=-1)
    x = _layernorm(x + _L1_gnn_ref(x, adj, L1_gnn_Wq, L1_gnn_bq, L1_gnn_Wk, L1_gnn_bk, L1_gnn_Wv, L1_gnn_bv, L1_gnn_beta), axis=-1)
    return x

_drawn_inputs = setup_inputs


def setup_inputs(seed=0):
    import zlib

    import numpy as np

    out = dict(_drawn_inputs(seed))
    spreads = {'L0_gnn_b_lin': (0.0, 0.1),
     'L0_gnn_ln_a': (1.0, 0.2),
     'L0_gnn_ln_b': (0.0, 0.1),
     'L1_gnn_bq': (0.0, 0.345),
     'L1_gnn_bk': (0.0, 0.8),
     'L1_gnn_bv': (0.0, 0.1)}
    factors = {}
    for name, (base, spread) in spreads.items():
        noise = np.random.default_rng([zlib.crc32(name.encode()), seed]).standard_normal(out[name].shape)
        drawn = base * np.exp(spread * noise) if base else spread * noise
        out[name] = jnp.asarray(drawn.astype(out[name].dtype))
    for name, factor in factors.items():
        out[name] = (out[name] * factor).astype(out[name].dtype)
    return out
```

```python
from contextlib import ExitStack

import numpy as np

import concourse.bass as bass
from concourse import mybir

ALU = mybir.AluOpType
ACT = mybir.ActivationFunctionType
AX = mybir.AxisListType
F32 = mybir.dt.float32
F32R = mybir.dt.float32r
F16 = mybir.dt.float16

P = 128
GRAPHS, NODES, FEAT = 16, 512, 384
NB = NODES // P
KB = FEAT // P
LAYERS = 2
HEADS = 12
HD = FEAT // HEADS
GROUP = P // HD
UNITS = NB * HEADS
HALF = HEADS // 2

W_SCALE = 64.0
P_SCALE = 1024.0
TEMPER = float(np.sqrt(FEAT))
SCORE_SCALE = W_SCALE * W_SCALE * float(np.sqrt(HD))
MASKED = -9000000000000000.0
LEFT, RIGHT, LIN = 0, 1, 2
W_Q, W_K, W_V = 6, 7, 8


def l0_steps():
    steps = []
    for l in range(LAYERS):
        steps += [("lin", l, 0), ("lin", l, 1), ("lin", l, 2)]
        steps += [("W", l, side, m) for side in (LEFT, RIGHT) for m in range(KB)]
        steps += [("u", l, 0), ("u", l, 1), ("u", l, 2), ("E", l, 0), ("u", l, 3), ("lin", l, 3), ("E", l, 1)]
        steps += [("E", l, 2), ("gap",), ("E", l, 3), ("gap",)]
        steps += [("ctx", l, i) for i in range(NB)]
        steps += [("norm", l), ("gap",), ("gap",)]
        if l == 1:
            steps += [("norm2",), ("gap",), ("gap",)]
        steps += [("T", l, k) for k in range(KB)]
        steps += [("gap",)]
    steps += [("W", 2, LEFT, m) for m in range(KB)] + [("W", 2, RIGHT, m) for m in range(KB)]
    steps += [("next_x",), ("select",)] + [("bias", i) for i in range(NB)]
    steps += [("v", j) for j in range(NB)]
    return steps


def attention_steps():
    slots = []
    for s in range(UNITS + 8):
        slot = []
        if s < UNITS:
            slot.append(("qk", s))
        if 1 <= s <= UNITS:
            slot.append(("t", s - 1))
        if 2 <= s <= UNITS + 1:
            slot.append(("pv", s - 2))
        for i in range(NB):
            last = HEADS * i + HEADS - 1
            if s == last - HALF + 3:
                slot.append(("reduce", i, 0))
            if s == last + 3:
                slot += [("reduce", i, 1), ("merge", i)]
            if s == last + 4:
                slot.append(("moments", i))
            if s == last + 6:
                slot.append(("finish", i))
        slots.append(slot)
    return slots


LONG = ("lin", "W", "u", "ctx", "gap")
LEAD = 3


def schedule(l0, attention):
    slots = attention_steps() if attention else []
    if not l0:
        return [step for slot in slots for step in slot]
    out, long_steps = [], 0
    for step in l0_steps():
        if step[0] == "W" and step[1] == 2 and step[2] == LEFT and step[3] == 0:
            for slot in slots:
                out += slot
            slots = []
        if step[0] != "gap":
            out.append(step)
        if step[0] in LONG:
            long_steps += 1
            if long_steps > LEAD and slots:
                out += slots.pop(0)
    return out


def work_fills():
    fills, f = {}, 0
    for step in l0_steps():
        if step[0] in ("lin", "W", "ctx", "T", "v"):
            fills[step], f = f, f + 1
        elif step[0] == "u":
            fills[step], f = f, f + 2
    return fills, f


FILL, FILLS = work_fills()
assert FILLS % 2 == 0
BANK_FILLS = FILLS // 2


def need(eng, sem, count):
    if isinstance(count, int) and count <= 0:
        return
    eng.wait_ge(sem, count)


def stand_alone(eng, passed):
    eng.sem_inc(passed, 1)


def graph_layers(nc, x, xT, adj, adjT, wl, wr, wlinT, b_lin, ln_a, ln_b, ln_a_by_block, ln_b_by_block,
                 wq, bq_by_block, wk, bk_by_block, wv, bv, beta, out):
    with ExitStack() as ctx:
        def sb(name, shape, dt):
            return ctx.enter_context(nc.sbuf_tensor(name, shape, dt))

        def bank(name):
            return ctx.enter_context(nc.psum_tensor(name, [P, 512], F32))

        def sem(name):
            return ctx.enter_context(nc.semaphore(name))

        w_hi = sb("w_hi", [P, 9, KB, FEAT], F16)
        w_lo = sb("w_lo", [P, 9, KB, FEAT], F16)
        ident = sb("ident", [P, P], F32)
        b_lin_rows = sb("b_lin_rows", [P, LAYERS, FEAT], F32)
        ln_a_rows = sb("ln_a_rows", [P, FEAT], F32)
        ln_b_rows = sb("ln_b_rows", [P, FEAT], F32)
        bv_rows = sb("bv_rows", [P, FEAT], F32)
        ln_a_col = sb("ln_a_col", [P, KB], F32)
        ln_b_col = sb("ln_b_col", [P, KB], F32)
        qk_bias = sb("qk_bias", [P, 2, KB], F32)
        beta_col = sb("beta_col", [P, 1], F32)
        half = sb("half", [P, NB], F32)
        minus_half = sb("minus_half", [P, NB], F32)
        norm_eps = sb("norm_eps", [P, NB], F32)
        x_nodes = sb("x_nodes", [P, NB, FEAT], F32)
        hT = sb("hT", [P, KB, NODES], F32)
        xa_hi = sb("xa_hi", [P, KB, NODES], F16)
        xa_lo = sb("xa_lo", [P, KB, NODES], F16)
        xb_hi = sb("xb_hi", [P, KB, NODES], F16)
        xb_lo = sb("xb_lo", [P, KB, NODES], F16)
        hw_hi = sb("hw_hi", [P, 2, KB, NODES], F16)
        hw_lo = sb("hw_lo", [P, 2, KB, NODES], F16)
        nat = sb("nat", [P, NB, FEAT + 2], F32)
        hl_hi = sb("hl_hi", [P, NB, FEAT + 2], F32R)
        hl_lo = sb("hl_lo", [P, NB, FEAT], F32R)
        adjT_sb = sb("adjT_sb", [P, NB, NODES], F32)
        edge = sb("edge", [P, NB, NODES], F32)
        edge_diag = sb("edge_diag", [P, NB, P], F32)
        diag_part = sb("diag_part", [P, P], F32)
        erow = sb("erow", [P, 3, NODES], F32)
        e_hi = sb("e_hi", [P, NB, NODES], F32R)
        e_lo = sb("e_lo", [P, NB, NODES], F32R)
        stats = sb("stats", [P, NB, 6], F32)
        moments = sb("moments", [P, NB, 2], F32)
        var_floor = sb("var_floor", [P, NB], F32)
        deviation = sb("deviation", [P, NB], F32)
        eps_sum = sb("eps_sum", [P, NB], F32)
        denom = sb("denom", [P, NB], F32)
        factor = sb("factor", [P, NB], F32)
        stats2 = sb("stats2", [P, NB, 6], F32)
        moments2 = sb("moments2", [P, NB, 2], F32)
        var2 = sb("var2", [P, NB], F32)
        factor2 = sb("factor2", [P, NB], F32)
        q_stack = sb("q_stack", [P, HEADS, NODES], F16)
        k_stack = sb("k_stack", [P, HEADS, NODES], F16)
        v_sb = sb("v_sb", [P, NB, HEADS, 2 * HD], F16)
        x2_bv = sb("x2_bv", [P, NB, FEAT], F32)
        bias = sb("bias", [P, NB, NODES], F32)
        masked = sb("masked", [P, NODES], F32)
        neg_scores = sb("neg_scores", [P, 2, NODES], F32)
        neg_max = sb("neg_max", [P, UNITS], F32)
        probs = sb("probs", [P, 2, NODES], F32)
        row_sum = sb("row_sum", [P, UNITS], F32)
        pT_hi = sb("pT_hi", [P, 2, NODES], F16)
        pT_lo = sb("pT_lo", [P, 2, NODES], F16)
        scaled_sum = sb("scaled_sum", [P, HEADS], F32)
        inv_sum = sb("inv_sum", [P, HEADS], F32)
        rows_out = sb("rows_out", [P, 2, FEAT], F32)
        stats3 = sb("stats3", [P, 6], F32)
        moments3 = sb("moments3", [P, 2], F32)
        var3 = sb("var3", [P, 1], F32)
        factor3 = sb("factor3", [P, 1], F32)

        work = [bank("work0"), bank("work1")]
        scores = [bank("scores0"), bank("scores1")]
        probsT = [bank("probsT0"), bank("probsT1")]
        heads_out = [bank("heads_out0"), bank("heads_out1")]

        weight_loaded = [sem(f"weight_loaded{i}") for i in range(4)]
        passed_sp, passed_dve, passed_pool = sem("passed_sp"), sem("passed_dve"), sem("passed_pool")
        weight_hi = sem("weight_hi")
        weight_lo = sem("weight_lo")
        consts_loaded = sem("consts_loaded")
        consts_scaled = sem("consts_scaled")
        pool_consts = sem("pool_consts")
        xT_loaded = sem("xT_loaded")
        x_loaded = sem("x_loaded")
        adjT_loaded = sem("adjT_loaded")
        edge_loaded = sem("edge_loaded")
        adj_loaded = sem("adj_loaded")
        selected = sem("selected")
        work_ready = sem("work_ready")
        emptied = [sem("emptied0"), sem("emptied1")]
        xa_hi_done = sem("xa_hi_done")
        xa_done = sem("xa_done")
        hi_done = sem("hi_done")
        xb_hi_done = sem("xb_hi_done")
        xb_done = sem("xb_done")
        hl_hi_done = sem("hl_hi_done")
        hl_lo_done = sem("hl_lo_done")
        z_done = sem("z_done")
        exp_done = sem("exp_done")
        e_done = sem("e_done")
        e_hi_done = sem("e_hi_done")
        e_lo_done = sem("e_lo_done")
        stats_done = sem("stats_done")
        moments_done = sem("moments_done")
        floor_done = sem("floor_done")
        deviation_done = sem("deviation_done")
        denom_done = sem("denom_done")
        factor_done = sem("factor_done")
        affine_done = sem("affine_done")
        stats2_done = sem("stats2_done")
        moments2_done = sem("moments2_done")
        var2_done = sem("var2_done")
        factor2_done = sem("factor2_done")
        normed = sem("normed")
        x2_bv_done = sem("x2_bv_done")
        masked_done = sem("masked_done")
        bias_done = sem("bias_done")
        stacked = sem("stacked")
        qk_done = sem("qk_done")
        max_done = sem("max_done")
        probs_done = sem("probs_done")
        probsT_done = sem("probsT_done")
        pT_hi_done = sem("pT_hi_done")
        pT_lo_done = sem("pT_lo_done")
        pv_done = sem("pv_done")
        reduced = sem("reduced")
        sum_scaled = sem("sum_scaled")
        sum_inverted = sem("sum_inverted")
        rows_scaled = sem("rows_scaled")
        rows_merged = sem("rows_merged")
        stats3_done = sem("stats3_done")
        moments3_done = sem("moments3_done")
        var3_done = sem("var3_done")
        factor3_done = sem("factor3_done")
        rows_done = sem("rows_done")
        stored = [sem("stored0"), sem("stored1")]

        HI_FILLS = [s for s in l0_steps() if s[0] in ("W", "v") or (s[0] == "T" and s[1] == 1)]
        HIS = len(HI_FILLS)
        LIN_ORDER = [s for s in l0_steps() if s[0] == "lin"]
        STACKS = 2 * 3 * GROUP

        def fill(step):
            f = FILL[step]
            return f, f % 2, f // 2

        stage = [q_stack[:, :, :].rearrange("p a b -> p (a b)")[:, i * 2 * KB * FEAT:(i + 1) * 2 * KB * FEAT].bitcast(F32)
                 for i in (0, 1)]
        stage += [k_stack[:, :, :].rearrange("p a b -> p (a b)")[:, i * 2 * KB * FEAT:(i + 1) * 2 * KB * FEAT].bitcast(F32)
                  for i in (0, 1)]
        w_dram = [wl[0], wr[0], wlinT[0], wl[1], wr[1], wlinT[1], wq, wk, wv]
        W_ORDER = [2, 0, 1, 5, 3, 4, 6, 7, 8]

        block = ctx.enter_context(nc.Block())

        @block.sync
        def _(sp):
            def load_weight(i):
                if i >= 4:
                    sp.wait_ge(weight_lo, i - 3)
                sp.dma_start(stage[i % 4].rearrange("p (c n) -> p c n", c=KB),
                             w_dram[W_ORDER[i]].rearrange("(c p) n -> p c n", p=P)).then_inc(weight_loaded[i % 4], 16)

            def load_xT(n):
                need(sp, xb_done, KB * n)
                stand_alone(sp, passed_sp)
                sp.dma_start(hT[:, :, :], xT[bass.ds(n, 1)].rearrange("a (c p) s -> p (a c) s", p=P)).then_inc(xT_loaded, 16)

            def load_x(n):
                need(sp, affine_done, 3 * NB * n)
                stand_alone(sp, passed_sp)
                sp.dma_start(x_nodes[:, :, :], x[bass.ds(n, 1)].rearrange("a (b p) f -> p (a b) f", p=P)).then_inc(x_loaded, 16)

            def load_adj_layer0(n):
                need(sp, e_done, LAYERS * NB * n)
                stand_alone(sp, passed_sp)
                sp.dma_start(adjT_sb[:, :, :], adjT[bass.ds(n, 1)].rearrange("a (b p) s -> p (a b) s", p=P)).then_inc(adjT_loaded, 16)
                for j in range(NB):
                    rows = slice(j * P, (j + 1) * P)
                    sp.dma_start(edge[:, j, j * P:], adj[bass.ds(n, 1), rows, j * P:].rearrange("a p s -> p (a s)")).then_inc(edge_loaded, 16)
                    if j:
                        sp.dma_start(edge[:, j, 0:j * P], adjT[bass.ds(n, 1), rows, 0:j * P].rearrange("a p s -> p (a s)")).then_inc(edge_loaded, 16)

            def load_bias(n):
                need(sp, max_done, UNITS * n)
                stand_alone(sp, passed_sp)
                sp.dma_start(bias[:, :, :], adj[bass.ds(n, 1)].rearrange("a (b p) s -> p (a b) s", p=P)).then_inc(adj_loaded, 16)

            def store(a, i):
                sp.wait_ge(rows_done, a * NB + i + 1)
                stand_alone(sp, passed_sp)
                sp.dma_start(out[bass.ds(a, 1), i * P:(i + 1) * P, :].rearrange("a p f -> p (a f)"),
                             rows_out[:, i % 2, :]).then_inc(stored[i % 2], 16)

            def stack(n, side):
                f, b, q = fill(("W", 2, side, KB - 1))
                sp.wait_ge(emptied[b], n * BANK_FILLS + q + 1)
                stand_alone(sp, passed_sp)
                f, b, q = fill(("W", 2, side, KB - 2))
                sp.wait_ge(emptied[b], n * BANK_FILLS + q + 1)
                stand_alone(sp, passed_sp)
                parts = (hw_hi, hw_hi, hw_lo) if side == LEFT else (hw_hi, hw_lo, hw_hi)
                dst = q_stack if side == LEFT else k_stack
                for slot, part in enumerate(parts):
                    for g in range(GROUP):
                        sp.dma_start(dst[HD * slot:HD * (slot + 1), g:HEADS:GROUP, :],
                                     part[HD * g:HD * (g + 1), side, :, :]).then_inc(stacked, 16)

            def turn(n, l0, attention):
                a = n - 1
                if attention:
                    store(a, 0)
                if l0:
                    load_xT(n + 1)
                if attention:
                    store(a, 1)
                    store(a, 2)
                if l0:
                    load_adj_layer0(n + 1)
                    load_x(n + 1)
                if attention:
                    store(a, 3)
                    for buffer in stored:
                        sp.wait_ge(buffer, 8 * NB * (a + 1))
                        stand_alone(sp, passed_sp)
                if l0:
                    load_bias(n)
                    stack(n, LEFT)
                    stack(n, RIGHT)

            load_xT(0)
            load_weight(0)
            load_weight(1)
            for dst, src in ((b_lin_rows[:, :, :], b_lin[:, :].partition_broadcast(P)),
                             (ln_a_rows[:, :], ln_a[1].partition_broadcast(P)),
                             (ln_b_rows[:, :], ln_b[1].partition_broadcast(P)),
                             (bv_rows[:, :], bv[:].partition_broadcast(P)),
                             (beta_col[:, :], beta[:].partition_broadcast(P)),
                             (ln_a_col[:, :], ln_a_by_block),
                             (ln_b_col[:, :], ln_b_by_block),
                             (qk_bias[:, 0, :], bq_by_block),
                             (qk_bias[:, 1, :], bk_by_block)):
                sp.dma_start(dst, src).then_inc(consts_loaded, 16)
            load_weight(2)
            load_adj_layer0(0)
            load_weight(3)
            load_x(0)
            for i in range(4, 9):
                load_weight(i)
            turn(0, True, False)
            with sp.Fori(1, GRAPHS) as n:
                turn(n, True, True)
            turn(GRAPHS, False, True)
            sp.wait_ge(xT_loaded, 16 * (GRAPHS + 1))
            sp.wait_ge(adjT_loaded, 16 * (GRAPHS + 1))
            sp.wait_ge(edge_loaded, 16 * (2 * NB - 1) * (GRAPHS + 1))
            sp.wait_ge(x_loaded, 16 * (GRAPHS + 1))
            sp.wait_ge(stored[0], 8 * NB * GRAPHS)
            sp.wait_ge(stored[1], 8 * NB * GRAPHS)

        @block.tensor
        def _(pe):
            def split_product(dst, lhs_hi, lhs_lo, rhs_hi, rhs_lo, ks):
                for k in ks:
                    for j, (a, b) in enumerate(((lhs_hi, rhs_hi), (lhs_hi, rhs_lo), (lhs_lo, rhs_hi))):
                        last = nc.tensor.matmul(dst, a(k), b(k), start=(k == ks[0] and j == 0),
                                                stop=(k == ks[-1] and j == 2))
                return last

            def bank_free(n, b, q):
                need(pe, emptied[b], n * BANK_FILLS + q)

            def emptied_all(n, step):
                f, b, q = fill(step)
                pe.wait_ge(emptied[b], n * BANK_FILLS + q + 1)
                pe.wait_ge(emptied[1 - b], n * BANK_FILLS + (f - 1) // 2 + 1)

            def layer_input(l):
                return (xa_hi, xa_lo) if l == 0 else (xb_hi, xb_lo)

            def lin(n, l, j):
                f, b, q = fill(("lin", l, j))
                if j == 0:
                    if l == 0:
                        pe.wait_ge(xa_done, n + 1)
                        if isinstance(n, int) and n == 0:
                            pe.wait_ge(weight_lo, 1)
                    else:
                        pe.wait_ge(xb_done, KB * (n + 1))
                        if isinstance(n, int) and n == 0:
                            pe.wait_ge(weight_lo, 4)
                hi, lo = layer_input(l)
                bank_free(n, b, q)
                rows = slice(j * P, (j + 1) * P)
                w = 3 * l + LIN
                split_product(work[b][:, 0:FEAT], lambda k: hi[:, k, rows], lambda k: lo[:, k, rows],
                              lambda k: w_hi[:, w, k, :], lambda k: w_lo[:, w, k, :],
                              range(KB)).then_inc(work_ready, 1)

            def W(n, l, side, m):
                f, b, q = fill(("W", l, side, m))
                if l == 2 and side == LEFT and m == 0:
                    emptied_all(n, ("T", 1, KB - 1))
                if isinstance(n, int) and n == 0 and m == 0:
                    pe.wait_ge(weight_lo, (2, 3, 5, 6, 7, 8)[2 * l + side])
                hi, lo = layer_input(l)
                bank_free(n, b, q)
                w = 3 * l + side
                cols = slice(m * P, (m + 1) * P)
                split_product(work[b][:, :], lambda k: w_hi[:, w, k, cols], lambda k: w_lo[:, w, k, cols],
                              lambda k: hi[:, k, :], lambda k: lo[:, k, :],
                              range(KB)).then_inc(work_ready, 1)

            def u(n, l, j):
                f, b, q = fill(("u", l, j))
                if j == 0:
                    emptied_all(n, ("W", l, RIGHT, KB - 1))
                hi, lo = layer_input(l)
                rows = slice(j * P, (j + 1) * P)
                for side, cols in ((LEFT, slice(0, (j + 1) * P)), (RIGHT, slice(j * P, NODES))):
                    bb, qq = (f + side) % 2, (f + side) // 2
                    bank_free(n, bb, qq)
                    split_product(work[bb][:, cols], lambda k: hi[:, k, rows], lambda k: lo[:, k, rows],
                                  lambda k: hw_hi[:, side, k, cols], lambda k: hw_lo[:, side, k, cols],
                                  range(KB)).then_inc(work_ready, 1)

            def ctx_rows(n, l, i):
                f, b, q = fill(("ctx", l, i))
                if i == 0:
                    pe.wait_ge(hl_lo_done, n * LAYERS * NB + (l + 1) * NB)
                    pe.wait_ge(e_lo_done, n * LAYERS * NB + (l + 1) * NB)
                bank_free(n, b, q)
                cols = slice(i * P, (i + 1) * P)
                for j in range(NB):
                    nc.tensor.matmul(work[b][:, 0:FEAT + 2], e_hi[:, j, cols], hl_hi[:, j, :], start=(j == 0), stop=False)
                    nc.tensor.matmul(work[b][:, 0:FEAT], e_hi[:, j, cols], hl_lo[:, j, :], start=False, stop=False)
                    last = nc.tensor.matmul(work[b][:, 0:FEAT + 2], e_lo[:, j, cols], hl_hi[:, j, :], start=False,
                                            stop=(j == NB - 1))
                last.then_inc(work_ready, 1)

            def transpose_rows(n, l, k):
                f, b, q = fill(("T", l, k))
                if k == 0:
                    pe.wait_ge(normed, n * LAYERS * NB + (l + 1) * NB)
                    if isinstance(n, int) and n == 0 and l == 0:
                        pe.wait_ge(pool_consts, 2)
                bank_free(n, b, q)
                for i in range(NB):
                    last = nc.tensor.transpose(work[b][:, i * P:(i + 1) * P], nat[:, i, k * P:(k + 1) * P], ident[:, :])
                last.then_inc(work_ready, 1)

            def v(n, j):
                f, b, q = fill(("v", j))
                if isinstance(n, int) and n == 0 and j == 0:
                    pe.wait_ge(weight_lo, 9)
                bank_free(n, b, q)
                rows = slice(j * P, (j + 1) * P)
                split_product(work[b][:, 0:FEAT], lambda k: xb_hi[:, k, rows], lambda k: xb_lo[:, k, rows],
                              lambda k: w_hi[:, W_V, k, :], lambda k: w_lo[:, W_V, k, :],
                              range(KB)).then_inc(work_ready, 1)

            def qk(a, s):
                i, h = divmod(s, HEADS)
                if s == 0:
                    pe.wait_ge(stacked, 16 * STACKS * (a + 1))
                else:
                    if s >= 2:
                        pe.wait_ge(max_done, a * UNITS + s - 1)
                nc.tensor.matmul(scores[s % 2][:, :], q_stack[0:3 * HD, h, i * P:(i + 1) * P], k_stack[0:3 * HD, h, :],
                                 start=True, stop=True).then_inc(qk_done, 1)

            def transpose_probs(a, s):
                pe.wait_ge(probs_done, a * UNITS + s + 1)
                if s >= 2:
                    pe.wait_ge(pT_lo_done, a * UNITS + s - 1)
                for j in range(NB):
                    last = nc.tensor.transpose(probsT[s % 2][:, j * P:(j + 1) * P], probs[:, s % 2, j * P:(j + 1) * P],
                                               ident[:, :])
                last.then_inc(probsT_done, 1)

            def pv(a, s):
                i, h = divmod(s, HEADS)
                b, c = divmod(h, HALF)
                pe.wait_ge(pT_lo_done, a * UNITS + s + 1)
                if s == 0:
                    pe.wait_ge(emptied[0], BANK_FILLS * (a + 1))
                    pe.wait_ge(emptied[1], BANK_FILLS * (a + 1))
                if c == 0 and i > 0:
                    pe.wait_ge(reduced, a * 2 * NB + 2 * (i - 1) + b + 1)
                cols = slice(c * 2 * HD, (c + 1) * 2 * HD)
                high = slice(c * 2 * HD, c * 2 * HD + HD)
                for j in range(NB):
                    nodes = slice(j * P, (j + 1) * P)
                    nc.tensor.matmul(heads_out[b][:, cols], pT_hi[:, s % 2, nodes], v_sb[:, j, h, :],
                                     start=(j == 0), stop=False)
                    last = nc.tensor.matmul(heads_out[b][:, high], pT_lo[:, s % 2, nodes], v_sb[:, j, h, 0:HD],
                                            start=False, stop=(j == NB - 1))
                last.then_inc(pv_done, 1)

            def turn(n, l0, attention):
                a = n - 1
                for step in schedule(l0, attention):
                    kind, at = step[0], step[1:]
                    if kind == "lin":
                        lin(n, *at)
                    elif kind == "W":
                        W(n, *at)
                    elif kind == "u":
                        u(n, *at)
                    elif kind == "ctx":
                        ctx_rows(n, *at)
                    elif kind == "T":
                        transpose_rows(n, *at)
                    elif kind == "v":
                        v(n, *at)
                    elif kind == "qk":
                        qk(a, *at)
                    elif kind == "t":
                        transpose_probs(a, *at)
                    elif kind == "pv":
                        pv(a, *at)

            turn(0, True, False)
            with pe.Fori(1, GRAPHS) as n:
                turn(n, True, True)
            turn(GRAPHS, False, True)

        @block.scalar
        def _(act):
            def split_x(n):
                act.wait_ge(xT_loaded, 16 * (n + 1))
                nc.scalar.copy(xa_hi[:, :, :], hT[:, :, :]).then_inc(xa_hi_done, 1)

            def fill_high(n, step, dst, b, f, bias_=None, src=None):
                act.wait_ge(work_ready, n * FILLS + f + 1)
                src = work[b][:, :] if src is None else src
                if bias_ is None:
                    nc.scalar.copy(dst, src).then_inc(hi_done, 1)
                else:
                    nc.scalar.activation(dst, src, ACT.Identity, bias=bias_).then_inc(hi_done, 1)

            def W(n, l, side, m):
                f, b, q = fill(("W", l, side, m))
                if l == 0 and side == LEFT and m == 0:
                    need(act, stacked, 16 * STACKS * n)
                fill_high(n, None, hw_hi[:, side, m, :], b, f, qk_bias[:, side, m:m + 1] if l == 2 else None)

            def lin(n, l, j):
                f, b, q = fill(("lin", l, j))
                act.wait_ge(emptied[b], n * BANK_FILLS + q + 1)
                nc.scalar.copy(hl_hi[:, j, 0:FEAT], nat[:, j, 0:FEAT]).then_inc(hl_hi_done, 1)

            def exp_row(n, l, j):
                act.wait_ge(z_done, n * LAYERS * NB + l * NB + j + 1)
                nc.scalar.activation(erow[:, j % 3, :], erow[:, j % 3, :], ACT.Exp).then_inc(exp_done, 1)

            def e_high(n, l, j):
                act.wait_ge(e_done, n * LAYERS * NB + l * NB + j + 1)
                nc.scalar.copy(e_hi[:, j, :], erow[:, j % 3, :]).then_inc(e_hi_done, 1)

            def ctx_rows(n, l, i):
                f, b, q = fill(("ctx", l, i))
                act.wait_ge(work_ready, n * FILLS + f + 1)
                nc.scalar.copy(nat[:, i, :], work[b][:, 0:FEAT + 2]).then_inc(emptied[b], 1)

            def transposed(n, l, k):
                f, b, q = fill(("T", l, k))
                if l == 0:
                    act.wait_ge(work_ready, n * FILLS + f + 1)
                    nc.scalar.activation(hT[:, k, :], work[b][:, :], ACT.Relu, bias=ln_b_col[:, k:k + 1],
                                         scale=ln_a_col[:, k:k + 1]).then_inc(emptied[b], 1)
                else:
                    fill_high(n, None, xb_hi[:, k, :], b, f)

            def v(n, j):
                f, b, q = fill(("v", j))
                fill_high(n, None, v_sb[:, j, :, 0:HD], b, f,
                          src=work[b][:, 0:FEAT].rearrange("p (h d) -> p h d", d=HD))

            def exp_scores(a, s):
                act.wait_ge(max_done, a * UNITS + s + 1)
                if s >= 2:
                    act.wait_ge(probsT_done, a * UNITS + s - 1)
                nc.scalar.activation(probs[:, s % 2, :], neg_scores[:, s % 2, :], ACT.Exp, bias=neg_max[:, s:s + 1],
                                     scale=-1.0, accum_out=row_sum[:, s:s + 1]).then_inc(probs_done, 1)

            def pT_high(a, s):
                act.wait_ge(probsT_done, a * UNITS + s + 1)
                if s >= 2:
                    act.wait_ge(pv_done, a * UNITS + s - 1)
                nc.scalar.mul(pT_hi[:, s % 2, :], probsT[s % 2][:, :], P_SCALE).then_inc(pT_hi_done, 1)

            def turn(n, l0, attention):
                a = n - 1
                for step in schedule(l0, attention):
                    kind, at = step[0], step[1:]
                    if kind == "next_x":
                        split_x(n + 1)
                    elif kind == "W":
                        W(n, *at)
                    elif kind == "lin":
                        lin(n, *at)
                    elif kind == "u":
                        exp_row(n, *at)
                    elif kind == "E":
                        e_high(n, *at)
                    elif kind == "ctx":
                        ctx_rows(n, *at)
                    elif kind == "T":
                        transposed(n, *at)
                    elif kind == "v":
                        v(n, *at)
                    elif kind == "qk":
                        exp_scores(a, *at)
                    elif kind == "t":
                        pT_high(a, *at)

            split_x(0)
            for i in range(9):
                act.wait_ge(weight_loaded[i % 4], 16 * (i // 4 + 1))
                nc.scalar.mul(w_hi[:, W_ORDER[i], :, :].rearrange("p c n -> p (c n)"), stage[i % 4],
                              W_SCALE).then_inc(weight_hi, 1)
                if i == 0:
                    act.wait_ge(consts_scaled, 1)
            turn(0, True, False)
            with act.Fori(1, GRAPHS) as n:
                turn(n, True, True)
            turn(GRAPHS, False, True)

        @block.vector
        def _(dve):
            def split_x(n):
                dve.wait_ge(xa_hi_done, n + 1)
                nc.vector.tensor_sub(xa_lo[:, :, :], hT[:, :, :], xa_hi[:, :, :]).then_inc(xa_done, 1)

            def hi_index(step):
                return HI_FILLS.index(step)

            def W(n, l, side, m):
                step = ("W", l, side, m)
                f, b, q = fill(step)
                dve.wait_ge(hi_done, n * HIS + hi_index(step) + 1)
                if l < 2:
                    nc.vector.tensor_sub(hw_lo[:, side, m, :], work[b][:, :], hw_hi[:, side, m, :]).then_inc(emptied[b], 1)
                else:
                    nc.vector.scalar_tensor_tensor(out=hw_lo[:, side, m, :], in0=work[b][:, :],
                                                   scalar=qk_bias[:, side, m:m + 1], in1=hw_hi[:, side, m, :],
                                                   op0=ALU.add, op1=ALU.subtract).then_inc(emptied[b], 1)

            def lin(n, l, j):
                f, b, q = fill(("lin", l, j))
                if l == 0 and j == 0:
                    need(dve, x2_bv_done, NB * n)
                dve.wait_ge(work_ready, n * FILLS + f + 1)
                nc.vector.scalar_tensor_tensor(out=nat[:, j, 0:FEAT], in0=work[b][:, 0:FEAT], scalar=1.0 / W_SCALE,
                                               in1=b_lin_rows[:, l, :], op0=ALU.mult, op1=ALU.add).then_inc(emptied[b], 1)

            def exponents(n, l, j):
                f = FILL[("u", l, j)]
                left, right = f % 2, (f + 1) % 2
                c = 1.0 / (W_SCALE * TEMPER)
                if l == 0 and j == 0:
                    dve.wait_ge(selected, n + 1)
                need(dve, z_done, n * LAYERS * NB + l * NB + j)
                need(dve, e_lo_done, n * LAYERS * NB + l * NB + max(j - 2, 0))
                dve.wait_ge(work_ready, n * FILLS + f + 1)
                if j:
                    nc.vector.scalar_tensor_tensor(out=erow[:, j % 3, 0:j * P], in0=work[left][:, 0:j * P], scalar=c,
                                                   in1=edge[:, j, 0:j * P], op0=ALU.mult, op1=ALU.mult)
                nc.vector.scalar_tensor_tensor(out=diag_part[:, :], in0=work[left][:, j * P:(j + 1) * P], scalar=c,
                                               in1=edge_diag[:, j, :], op0=ALU.mult, op1=ALU.mult).then_inc(emptied[left], 1)
                dve.wait_ge(work_ready, n * FILLS + f + 2)
                nc.vector.scalar_tensor_tensor(out=erow[:, j % 3, j * P:], in0=work[right][:, j * P:], scalar=c,
                                               in1=edge[:, j, j * P:], op0=ALU.mult, op1=ALU.mult).then_inc(emptied[right], 1)
                dve.wait_ge(emptied[right], n * BANK_FILLS + (f + 1) // 2 + 1)
                nc.vector.tensor_add(erow[:, j % 3, j * P:(j + 1) * P], erow[:, j % 3, j * P:(j + 1) * P],
                                     diag_part[:, :]).then_inc(z_done, 1)

            def e_low(n, l, j):
                dve.wait_ge(e_hi_done, n * LAYERS * NB + l * NB + j + 1)
                nc.vector.tensor_sub(e_lo[:, j, :], erow[:, j % 3, :], e_hi[:, j, :].bitcast(F32)).then_inc(e_lo_done, 1)

            def ctx_rows(n, l, i):
                f, b, q = fill(("ctx", l, i))
                dve.wait_ge(emptied[b], n * BANK_FILLS + q + 1)
                nc.vector.bn_stats(stats[:, i, :], nat[:, i, 0:FEAT]).then_inc(stats_done, 1)

            def norm(n, l):
                per = n * LAYERS + l
                dve.wait_ge(stats_done, n * LAYERS * NB + (l + 1) * NB)
                stand_alone(dve, passed_dve)
                for i in range(NB):
                    last = nc.vector.bn_aggr(moments[:, i, :], stats[:, i, :])
                last.then_inc(moments_done, 1)
                nc.vector.tensor_scalar(eps_sum[:, :], nat[:, :, FEAT], 1e-10, 1e-3, ALU.add, ALU.mult)
                dve.wait_ge(moments_done, per + 1)
                nc.vector.tensor_scalar(var_floor[:, :], moments[:, :, 1], 1e-36, None, ALU.max).then_inc(floor_done, 1)
                dve.wait_ge(deviation_done, per + 1)
                nc.vector.scalar_tensor_tensor(out=denom[:, :], in0=deviation[:, :],
                                               scalar=float(np.sqrt(FEAT / (FEAT - 1.0))), in1=eps_sum[:, :],
                                               op0=ALU.mult, op1=ALU.add).then_inc(denom_done, 1)
                dve.wait_ge(denom_done, per + 1)
                nc.vector.reciprocal(factor[:, :], denom[:, :]).then_inc(factor_done, 1)
                dve.wait_ge(factor_done, per + 1)
                if l == 0:
                    for i in range(NB):
                        nc.vector.tensor_scalar(nat[:, i, 0:FEAT], nat[:, i, 0:FEAT], moments[:, i, 0:1],
                                                factor[:, i:i + 1], ALU.subtract, ALU.mult).then_inc(normed, 1)
                    return
                for i in range(NB):
                    nc.vector.scalar_tensor_tensor(out=nat[:, i, 0:FEAT], in0=nat[:, i, 0:FEAT], scalar=moments[:, i, 0:1],
                                                   in1=ln_a_rows[:, :], op0=ALU.subtract, op1=ALU.mult).then_inc(affine_done, 1)
                for i in range(NB):
                    dve.wait_ge(affine_done, n * 3 * NB + i + 1)
                    nc.vector.scalar_tensor_tensor(out=nat[:, i, 0:FEAT], in0=nat[:, i, 0:FEAT], scalar=factor[:, i:i + 1],
                                                   in1=ln_b_rows[:, :], op0=ALU.mult, op1=ALU.add).then_inc(affine_done, 1)
                dve.wait_ge(x_loaded, 16 * (n + 1))
                for i in range(NB):
                    dve.wait_ge(affine_done, n * 3 * NB + NB + i + 1)
                    nc.vector.scalar_tensor_tensor(out=nat[:, i, 0:FEAT], in0=nat[:, i, 0:FEAT], scalar=0.0,
                                                   in1=x_nodes[:, i, :], op0=ALU.max, op1=ALU.add).then_inc(affine_done, 1)
                for i in range(NB):
                    dve.wait_ge(affine_done, n * 3 * NB + 2 * NB + i + 1)
                    nc.vector.bn_stats(stats2[:, i, :], nat[:, i, 0:FEAT]).then_inc(stats2_done, 1)
                dve.wait_ge(stats2_done, (n + 1) * NB)
                stand_alone(dve, passed_dve)
                for i in range(NB):
                    last = nc.vector.bn_aggr(moments2[:, i, :], stats2[:, i, :])
                last.then_inc(moments2_done, 1)

            def norm2(n):
                dve.wait_ge(factor2_done, n + 1)
                for i in range(NB):
                    nc.vector.tensor_scalar(nat[:, i, 0:FEAT], nat[:, i, 0:FEAT], moments2[:, i, 0:1],
                                            factor2[:, i:i + 1], ALU.subtract, ALU.mult).then_inc(normed, 1)

            def transposed(n, l, k):
                step = ("T", l, k)
                f, b, q = fill(step)
                if l == 0:
                    dve.wait_ge(emptied[b], n * BANK_FILLS + q + 1)
                    nc.vector.tensor_copy(xb_hi[:, k, :], hT[:, k, :]).then_inc(xb_hi_done, 1)
                    dve.wait_ge(xb_hi_done, n * KB + k + 1)
                    nc.vector.tensor_sub(xb_lo[:, k, :], hT[:, k, :], xb_hi[:, k, :]).then_inc(xb_done, 1)
                else:
                    dve.wait_ge(hi_done, n * HIS + hi_index(step) + 1)
                    nc.vector.tensor_sub(xb_lo[:, k, :], work[b][:, :], xb_hi[:, k, :]).then_inc(emptied[b], 1)

            def make_bias(n, i):
                dve.wait_ge(adj_loaded, 16 * (n + 1))
                need(dve, bias_done, n * NB + i)
                nc.vector.tensor_scalar(masked[:, :], bias[:, i, :], 0.0, MASKED * SCORE_SCALE, ALU.is_le,
                                        ALU.mult).then_inc(masked_done, 1)
                dve.wait_ge(masked_done, n * NB + i + 1)
                nc.vector.scalar_tensor_tensor(out=bias[:, i, :], in0=bias[:, i, :], scalar=beta_col[:, 0:1],
                                               in1=masked[:, :], op0=ALU.mult, op1=ALU.add).then_inc(bias_done, 1)

            def v(n, j):
                step = ("v", j)
                f, b, q = fill(step)
                dve.wait_ge(hi_done, n * HIS + hi_index(step) + 1)
                nc.vector.tensor_sub(v_sb[:, j, :, HD:2 * HD], work[b][:, 0:FEAT].rearrange("p (h d) -> p h d", d=HD),
                                     v_sb[:, j, :, 0:HD]).then_inc(emptied[b], 1)

            def masked_scores(a, s):
                i, h = divmod(s, HEADS)
                if s == 0:
                    dve.wait_ge(bias_done, NB * (a + 1))
                dve.wait_ge(qk_done, a * UNITS + s + 1)
                if s >= 2:
                    dve.wait_ge(probs_done, a * UNITS + s - 1)
                stand_alone(dve, passed_dve)
                nc.vector.tensor_tensor_reduce(out=neg_scores[:, s % 2, :], in0=scores[s % 2][:, :], in1=bias[:, i, :],
                                               scale=-1.0 / SCORE_SCALE, scalar=3.0e38, op0=ALU.add, op1=ALU.min,
                                               accum_out=neg_max[:, s:s + 1]).then_inc(max_done, 1)

            def pT_low(a, s):
                dve.wait_ge(pT_hi_done, a * UNITS + s + 1)
                nc.vector.scalar_tensor_tensor(out=pT_lo[:, s % 2, :], in0=probsT[s % 2][:, :], scalar=P_SCALE,
                                               in1=pT_hi[:, s % 2, :], op0=ALU.mult, op1=ALU.subtract).then_inc(pT_lo_done, 1)

            def reduce(a, i, b):
                dve.wait_ge(pv_done, a * UNITS + HEADS * i + HALF * (b + 1))
                if i >= 2:
                    dve.wait_ge(stored[i % 2], 16 * (a * (NB // 2) + 1))
                nc.vector.tensor_reduce(
                    rows_out[:, i % 2, b * HALF * HD:(b + 1) * HALF * HD].rearrange("p (h d) -> p h d", d=HD),
                    heads_out[b][:, 0:HALF * 2 * HD].rearrange("p (h e d) -> p h d e", e=2, d=HD),
                    axis=AX.X, op=ALU.add).then_inc(reduced, 1)

            def merge(a, i):
                dve.wait_ge(probs_done, a * UNITS + HEADS * (i + 1))
                need(dve, rows_scaled, a * NB + i)
                nc.vector.tensor_scalar(scaled_sum[:, :], row_sum[:, HEADS * i:HEADS * (i + 1)], W_SCALE * P_SCALE, None,
                                        ALU.mult).then_inc(sum_scaled, 1)
                dve.wait_ge(sum_scaled, a * NB + i + 1)
                nc.vector.reciprocal(inv_sum[:, :], scaled_sum[:, :]).then_inc(sum_inverted, 1)

            def moments_of_rows(a, i):
                dve.wait_ge(rows_merged, a * NB + i + 1)
                need(dve, rows_done, a * NB + i)
                nc.vector.bn_stats(stats3[:, :], rows_out[:, i % 2, :]).then_inc(stats3_done, 1)
                dve.wait_ge(stats3_done, a * NB + i + 1)
                stand_alone(dve, passed_dve)
                nc.vector.bn_aggr(moments3[:, :], stats3[:, :]).then_inc(moments3_done, 1)

            def finish(a, i):
                dve.wait_ge(factor3_done, a * NB + i + 1)
                nc.vector.tensor_scalar(rows_out[:, i % 2, :], rows_out[:, i % 2, :], moments3[:, 0:1], factor3[:, 0:1],
                                        ALU.subtract, ALU.mult).then_inc(rows_done, 1)

            def turn(n, l0, attention):
                a = n - 1
                for step in schedule(l0, attention):
                    kind, at = step[0], step[1:]
                    if kind == "next_x":
                        split_x(n + 1)
                    elif kind == "W":
                        W(n, *at)
                    elif kind == "lin":
                        lin(n, *at)
                    elif kind == "u":
                        exponents(n, *at)
                    elif kind == "E":
                        e_low(n, *at)
                    elif kind == "ctx":
                        ctx_rows(n, *at)
                    elif kind == "norm":
                        norm(n, *at)
                    elif kind == "norm2":
                        norm2(n)
                    elif kind == "T":
                        transposed(n, *at)
                    elif kind == "bias":
                        make_bias(n, *at)
                    elif kind == "v":
                        v(n, *at)
                    elif kind == "qk":
                        masked_scores(a, *at)
                    elif kind == "t":
                        pT_low(a, *at)
                    elif kind == "reduce":
                        reduce(a, *at)
                    elif kind == "merge":
                        merge(a, *at)
                    elif kind == "moments":
                        moments_of_rows(a, *at)
                    elif kind == "finish":
                        finish(a, *at)

            nc.vector.memset(hl_hi[:, :, FEAT:FEAT + 2].bitcast(F32), 1.0)
            split_x(0)
            dve.wait_ge(consts_loaded, 16 * 9)
            nc.vector.tensor_scalar(beta_col[:, :], beta_col[:, :], SCORE_SCALE, None, ALU.mult)
            nc.vector.tensor_scalar(qk_bias[:, :, :], qk_bias[:, :, :], W_SCALE, None, ALU.mult).then_inc(consts_scaled, 1)
            for i in range(9):
                dve.wait_ge(weight_hi, i + 1)
                nc.vector.scalar_tensor_tensor(out=w_lo[:, W_ORDER[i], :, :].rearrange("p c n -> p (c n)"), in0=stage[i % 4],
                                               scalar=W_SCALE, in1=w_hi[:, W_ORDER[i], :, :].rearrange("p c n -> p (c n)"),
                                               op0=ALU.mult, op1=ALU.subtract).then_inc(weight_lo, 1)
            dve.wait_ge(consts_scaled, 1)
            turn(0, True, False)
            with dve.Fori(1, GRAPHS) as n:
                turn(n, True, True)
            turn(GRAPHS, False, True)

        @block.gpsimd
        def _(pool):
            def select(n):
                pool.wait_ge(adjT_loaded, 16 * (n + 1))
                pool.wait_ge(edge_loaded, 16 * (2 * NB - 1) * (n + 1))
                stand_alone(pool, passed_pool)
                for j in range(NB):
                    cols = slice(j * P, (j + 1) * P)
                    nc.gpsimd.affine_select(out=edge_diag[:, j, :], in_=adjT_sb[:, j, cols], compare_op=ALU.is_ge,
                                            fill=0.0, base=0, pattern=[[-1, P]], channel_multiplier=1)
                    last = nc.gpsimd.affine_select(out=edge[:, j, cols], in_=edge[:, j, cols], compare_op=ALU.is_gt,
                                                   fill=0.0, base=0, pattern=[[1, P]], channel_multiplier=-1)
                last.then_inc(selected, 1)

            def hl_low(n, l, j):
                pool.wait_ge(hl_hi_done, n * LAYERS * NB + l * NB + j + 1)
                nc.gpsimd.tensor_sub(hl_lo[:, j, :], nat[:, j, 0:FEAT], hl_hi[:, j, 0:FEAT].bitcast(F32)).then_inc(hl_lo_done, 1)

            def times_adj(n, l, j):
                pool.wait_ge(exp_done, n * LAYERS * NB + l * NB + j + 1)
                nc.gpsimd.tensor_mul(erow[:, j % 3, :], erow[:, j % 3, :], adjT_sb[:, j, :]).then_inc(e_done, 1)

            def norm(n, l):
                pool.wait_ge(floor_done, n * LAYERS + l + 1)
                nc.gpsimd.tensor_tensor(deviation[:, :], var_floor[:, :], half[:, :], ALU.pow).then_inc(deviation_done, 1)
                if l == 1:
                    pool.wait_ge(moments2_done, n + 1)
                    nc.gpsimd.tensor_add(var2[:, :], moments2[:, :, 1], norm_eps[:, :]).then_inc(var2_done, 1)
                    pool.wait_ge(var2_done, n + 1)
                    nc.gpsimd.tensor_tensor(factor2[:, :], var2[:, :], minus_half[:, :], ALU.pow).then_inc(factor2_done, 1)

            def residual(n):
                pool.wait_ge(normed, n * LAYERS * NB + 2 * NB)
                for i in range(NB):
                    nc.gpsimd.tensor_add(x2_bv[:, i, :], nat[:, i, 0:FEAT], bv_rows[:, :]).then_inc(x2_bv_done, 1)

            def merge(a, i):
                pool.wait_ge(sum_inverted, a * NB + i + 1)
                pool.wait_ge(reduced, a * 2 * NB + 2 * i + 2)
                rows = rows_out[:, i % 2, :].rearrange("p (h d) -> p h d", d=HD)
                nc.gpsimd.tensor_tensor(rows, rows, inv_sum[:, :].unsqueeze(2).to_broadcast([P, HEADS, HD]),
                                        ALU.mult).then_inc(rows_scaled, 1)
                pool.wait_ge(rows_scaled, a * NB + i + 1)
                nc.gpsimd.tensor_add(rows_out[:, i % 2, :], rows_out[:, i % 2, :], x2_bv[:, i, :]).then_inc(rows_merged, 1)

            def factor_of_rows(a, i):
                pool.wait_ge(moments3_done, a * NB + i + 1)
                nc.gpsimd.tensor_add(var3[:, :], moments3[:, 1:2], norm_eps[:, 0:1]).then_inc(var3_done, 1)
                pool.wait_ge(var3_done, a * NB + i + 1)
                nc.gpsimd.tensor_tensor(factor3[:, :], var3[:, :], minus_half[:, 0:1], ALU.pow).then_inc(factor3_done, 1)

            def turn(n, l0, attention):
                a = n - 1
                for step in schedule(l0, attention):
                    kind, at = step[0], step[1:]
                    if kind == "select":
                        residual(n)
                        select(n + 1)
                    elif kind == "lin":
                        hl_low(n, *at)
                    elif kind == "u":
                        times_adj(n, *at)
                    elif kind == "norm":
                        norm(n, *at)
                    elif kind == "merge":
                        merge(a, *at)
                    elif kind == "moments":
                        factor_of_rows(a, *at)

            nc.gpsimd.memset(half[:, :], 0.5)
            nc.gpsimd.memset(minus_half[:, :], -0.5)
            nc.gpsimd.memset(norm_eps[:, :], 1e-5)
            nc.gpsimd.memset(ident[:, :], 0.0).then_inc(pool_consts, 1)
            pool.wait_ge(pool_consts, 1)
            nc.gpsimd.affine_select(out=ident[:, :], in_=ident[:, :], compare_op=ALU.not_equal, fill=1.0, base=0,
                                    pattern=[[-1, P]], channel_multiplier=1).then_inc(pool_consts, 1)
            pool.wait_ge(consts_loaded, 16 * 9)
            select(0)
            turn(0, True, False)
            with pool.Fori(1, GRAPHS) as n:
                turn(n, True, True)
            turn(GRAPHS, False, True)


def kernel(**inputs):
    import concourse.bacc as bacc
    from concourse.bass_utils import run_bass_kernel_spmd

    def one_more(a):
        return np.concatenate([a, a[:1]])

    def by_block(a):
        return np.asarray(a).reshape(KB, P).T

    x = np.asarray(inputs["x"])
    adj = np.asarray(inputs["adj"])
    arrays = {
        "x": one_more(x),
        "xT": one_more(x.transpose(0, 2, 1)),
        "adj": one_more(adj),
        "adjT": one_more(adj.transpose(0, 2, 1)),
        "wl": inputs["L0_gnn_W_left"],
        "wr": inputs["L0_gnn_W_right"],
        "wlinT": np.asarray(inputs["L0_gnn_W_lin"]).transpose(0, 2, 1),
        "b_lin": inputs["L0_gnn_b_lin"],
        "ln_a": inputs["L0_gnn_ln_a"],
        "ln_b": inputs["L0_gnn_ln_b"],
        "ln_a_by_block": by_block(inputs["L0_gnn_ln_a"][0]),
        "ln_b_by_block": by_block(inputs["L0_gnn_ln_b"][0]),
        "wq": inputs["L1_gnn_Wq"],
        "bq_by_block": by_block(inputs["L1_gnn_bq"]),
        "wk": inputs["L1_gnn_Wk"],
        "bk_by_block": by_block(inputs["L1_gnn_bk"]),
        "wv": inputs["L1_gnn_Wv"],
        "bv": inputs["L1_gnn_bv"],
        "beta": np.asarray(inputs["L1_gnn_beta"]).reshape(1),
    }
    arrays = {f"in_{k}": np.ascontiguousarray(v) for k, v in arrays.items()}
    nc = bacc.Bacc("TRN2", target_bir_lowering=False, num_devices=1)
    args = [nc.dram_tensor(k, v.shape, mybir.dt.from_np(v.dtype), kind="ExternalInput").ap() for k, v in arrays.items()]
    out = nc.dram_tensor("out_0", (GRAPHS, NODES, FEAT), F32, kind="ExternalOutput").ap()
    graph_layers(nc, *args, out)
    r = run_bass_kernel_spmd(nc, [arrays], core_ids=[0])
    return r.results[0]["out_0"]
```

```python
from contextlib import ExitStack

import numpy as np

import concourse.bass as bass
from concourse import mybir

ALU = mybir.AluOpType
ACT = mybir.ActivationFunctionType
AX = mybir.AxisListType
F32 = mybir.dt.float32
F32R = mybir.dt.float32r
F16 = mybir.dt.float16

P = 128
GRAPHS, NODES, FEAT = 16, 512, 384
NB = NODES // P
KB = FEAT // P
LAYERS = 2
HEADS = 12
HD = FEAT // HEADS
GROUP = P // HD
UNITS = NB * HEADS
HALF = HEADS // 2

W_SCALE = 64.0
P_SCALE = 1024.0
TEMPER = float(np.sqrt(FEAT))
SCORE_SCALE = W_SCALE * W_SCALE * float(np.sqrt(HD))
MASKED = -9000000000000000.0
LEFT, RIGHT, LIN = 0, 1, 2
W_Q, W_K, W_V = 6, 7, 8


def l0_steps():
    steps = []
    for l in range(LAYERS):
        steps += [(("lin", l, j), 0.7 * l) for j in range(3)]
        steps += [(("W", l, side, m), 0.8) for side in (LEFT, RIGHT) for m in range(KB)]
        steps += [(("u", l, 0), 1), (("u", l, 1), 1), (("u", l, 2), 1), (("E", l, 0), 0), (("u", l, 3), 1),
                  (("E", l, 1), 0), (("lin", l, 3), 1), (("E", l, 2), 1.5), (("E", l, 3), 1.5)]
        steps += [(("ctx", l, i), 0.75) for i in range(NB)]
        steps += [(("moments0", l), 1), (("norm", l), 1)]
        if l == 1:
            steps += [(("relu", i), 1.5) for i in range(NB)]
            steps += [(("moments2",), 1), (("norm2",), 1.5)]
        steps += [(("T", l, k), 0.5) for k in range(KB)]
        steps += [(("next",), 2)]
    steps += [(("W", 2, LEFT, m), 1) for m in range(KB)] + [(("W", 2, RIGHT, m), 0) for m in range(KB)]
    steps += [(("next_x",), 0), (("select",), 0)] + [(("bias", i), 0) for i in range(NB)]
    steps += [(("v", j), 0) for j in range(NB)]
    return steps


def attention_steps():
    slots = []
    for s in range(UNITS + 8):
        slot = []
        for kind, lag in (("qk", 0), ("exp", 1), ("t", 2), ("low_t", 3), ("pv", V_LAG)):
            if lag <= s < UNITS + lag:
                slot.append((kind, s - lag))
        for i in range(NB):
            ends = HEADS * (i + 1) + V_LAG
            if s == ends - HALF:
                slot.append(("reduce", i, 0))
            if s == ends:
                slot += [("reduce", i, 1), ("merge", i)]
            if s == ends + 2:
                slot.append(("moments", i))
            if s == ends + 3:
                slot.append(("finish", i))
        slots.append(slot)
    return slots


V_LAG = 4
DEPTH = 3


def schedule(l0, attention):
    slots = attention_steps() if attention else []
    if not l0:
        return [step for slot in slots for step in slot]
    out, due = [], 0.0
    for step, count in l0_steps():
        if step == ("W", 2, RIGHT, 0):
            out += [x for slot in slots for x in slot]
            slots = []
        out.append(step)
        due += count
        while due >= 1 and slots:
            out += slots.pop(0)
            due -= 1
        out.append(("after",) + step)
    return out


def work_fills():
    fills, f = {}, 0
    for step, _ in l0_steps():
        if step[0] in ("lin", "W", "ctx", "T", "v"):
            fills[step], f = f, f + 1
        elif step[0] == "u":
            fills[step], f = f, f + 2
    return fills, f


FILL, FILLS = work_fills()
assert FILLS % 2 == 0
BANK_FILLS = FILLS // 2


def need(eng, sem, count):
    if isinstance(count, int) and count <= 0:
        return
    eng.wait_ge(sem, count)


def stand_alone(eng, passed):
    eng.sem_inc(passed, 1)


def graph_layers(nc, x, xT, adj, adjT, wl, wr, wlinT, b_lin, ln_a, ln_b, ln_a_by_block, ln_b_by_block,
                 wq, bq_by_block, wk, bk_by_block, wv, bv, beta, out):
    with ExitStack() as ctx:
        def sb(name, shape, dt):
            return ctx.enter_context(nc.sbuf_tensor(name, shape, dt))

        def bank(name):
            return ctx.enter_context(nc.psum_tensor(name, [P, 512], F32))

        def sem(name):
            return ctx.enter_context(nc.semaphore(name))

        w_hi = sb("w_hi", [P, 9, KB, FEAT], F16)
        w_lo = sb("w_lo", [P, 9, KB, FEAT], F16)
        ident = sb("ident", [P, P], F32)
        b_lin_rows = sb("b_lin_rows", [P, LAYERS, FEAT], F32)
        ln_a_rows = sb("ln_a_rows", [P, FEAT], F32)
        ln_b_rows = sb("ln_b_rows", [P, FEAT], F32)
        bv_rows = sb("bv_rows", [P, FEAT], F32)
        ln_a_col = sb("ln_a_col", [P, KB], F32)
        ln_b_col = sb("ln_b_col", [P, KB], F32)
        qk_bias = sb("qk_bias", [P, 2, KB], F32)
        beta_col = sb("beta_col", [P, 1], F32)
        half = sb("half", [P, NB], F32)
        minus_half = sb("minus_half", [P, NB], F32)
        norm_eps = sb("norm_eps", [P, NB], F32)
        x_nodes = sb("x_nodes", [P, NB, FEAT], F32)
        hT = sb("hT", [P, KB, NODES], F32)
        xa_hi = sb("xa_hi", [P, KB, NODES], F16)
        xa_lo = sb("xa_lo", [P, KB, NODES], F16)
        xb_hi = sb("xb_hi", [P, KB, NODES], F16)
        xb_lo = sb("xb_lo", [P, KB, NODES], F16)
        hw_hi = sb("hw_hi", [P, 2, KB, NODES], F16)
        hw_lo = sb("hw_lo", [P, 2, KB, NODES], F16)
        nat = sb("nat", [P, NB, FEAT + 2], F32)
        hl_hi = sb("hl_hi", [P, NB, FEAT + 2], F32R)
        hl_lo = sb("hl_lo", [P, NB, FEAT], F32R)
        adjT_sb = sb("adjT_sb", [P, NB, NODES], F32)
        edge = sb("edge", [P, NB, NODES], F32)
        edge_diag = sb("edge_diag", [P, NB, P], F32)
        diag_part = sb("diag_part", [P, P], F32)
        erow = sb("erow", [P, 3, NODES], F32)
        e_hi = sb("e_hi", [P, NB, NODES], F32R)
        e_lo = sb("e_lo", [P, NB, NODES], F32R)
        stats = sb("stats", [P, NB, 6], F32)
        moments = sb("moments", [P, NB, 2], F32)
        var_floor = sb("var_floor", [P, NB], F32)
        deviation = sb("deviation", [P, NB], F32)
        eps_sum = sb("eps_sum", [P, NB], F32)
        denom = sb("denom", [P, NB], F32)
        factor = sb("factor", [P, NB], F32)
        stats2 = sb("stats2", [P, NB, 6], F32)
        moments2 = sb("moments2", [P, NB, 2], F32)
        var2 = sb("var2", [P, NB], F32)
        factor2 = sb("factor2", [P, NB], F32)
        q_stack = sb("q_stack", [P, HEADS, NODES], F16)
        k_stack = sb("k_stack", [P, HEADS, NODES], F16)
        v_sb = sb("v_sb", [P, NB, HEADS, 2 * HD], F16)
        x2_bv = sb("x2_bv", [P, NB, FEAT], F32)
        bias = sb("bias", [P, NB, NODES], F32)
        neg_scores = sb("neg_scores", [P, 2, NODES], F32)
        masked = neg_scores[:, 0, :]
        neg_max = sb("neg_max", [P, UNITS], F32)
        probs = sb("probs", [P, DEPTH, NODES], F32)
        row_sum = sb("row_sum", [P, UNITS], F32)
        pT_hi = sb("pT_hi", [P, DEPTH, NODES], F16)
        pT_lo = sb("pT_lo", [P, DEPTH, NODES], F16)
        scaled_sum = sb("scaled_sum", [P, HEADS], F32)
        inv_sum = sb("inv_sum", [P, HEADS], F32)
        rows_out = sb("rows_out", [P, 2, FEAT], F32)
        stats3 = sb("stats3", [P, 6], F32)
        moments3 = sb("moments3", [P, 2], F32)
        var3 = sb("var3", [P, 1], F32)
        factor3 = sb("factor3", [P, 1], F32)

        work = [bank("work0"), bank("work1")]
        scores = [bank("scores0"), bank("scores1")]
        probsT = [bank("probsT0"), bank("probsT1")]
        heads_out = [bank("heads_out0"), bank("heads_out1")]

        weight_loaded = [sem(f"weight_loaded{i}") for i in range(4)]
        passed_sp, passed_dve, passed_pool = sem("passed_sp"), sem("passed_dve"), sem("passed_pool")
        weight_hi = sem("weight_hi")
        weight_lo = sem("weight_lo")
        consts_loaded = sem("consts_loaded")
        consts_scaled = sem("consts_scaled")
        pool_consts = sem("pool_consts")
        xT_loaded = sem("xT_loaded")
        x_loaded = sem("x_loaded")
        adjT_loaded = sem("adjT_loaded")
        edge_loaded = sem("edge_loaded")
        adj_loaded = sem("adj_loaded")
        selected = sem("selected")
        work_ready = sem("work_ready")
        emptied = [sem("emptied0"), sem("emptied1")]
        xa_hi_done = sem("xa_hi_done")
        xa_done = sem("xa_done")
        hi_done = sem("hi_done")
        xb_hi_done = sem("xb_hi_done")
        xb_done = sem("xb_done")
        hl_hi_done = sem("hl_hi_done")
        hl_lo_done = sem("hl_lo_done")
        z_done = sem("z_done")
        exp_done = sem("exp_done")
        e_done = sem("e_done")
        e_hi_done = sem("e_hi_done")
        e_lo_done = sem("e_lo_done")
        stats_done = sem("stats_done")
        moments_done = sem("moments_done")
        floor_done = sem("floor_done")
        deviation_done = sem("deviation_done")
        denom_done = sem("denom_done")
        factor_done = sem("factor_done")
        scaled = sem("scaled")
        times_a = sem("times_a")
        affine_done = sem("affine_done")
        residual_done = sem("residual_done")
        stats2_done = sem("stats2_done")
        moments2_done = sem("moments2_done")
        var2_done = sem("var2_done")
        factor2_done = sem("factor2_done")
        normed = sem("normed")
        x2_bv_done = sem("x2_bv_done")
        masked_done = sem("masked_done")
        bias_done = sem("bias_done")
        stacked = sem("stacked")
        qk_done = sem("qk_done")
        max_done = sem("max_done")
        probs_done = sem("probs_done")
        probsT_done = sem("probsT_done")
        pT_hi_done = sem("pT_hi_done")
        pT_lo_done = sem("pT_lo_done")
        pv_done = sem("pv_done")
        reduced = sem("reduced")
        sum_scaled = sem("sum_scaled")
        sum_inverted = sem("sum_inverted")
        rows_scaled = sem("rows_scaled")
        rows_merged = sem("rows_merged")
        stats3_done = sem("stats3_done")
        moments3_done = sem("moments3_done")
        var3_done = sem("var3_done")
        factor3_done = sem("factor3_done")
        rows_done = sem("rows_done")
        stored = [sem("stored0"), sem("stored1")]

        HI_FILLS = [s for s, _ in l0_steps() if s[0] in ("W", "v") or (s[0] == "T" and s[1] == 1)]
        HIS = len(HI_FILLS)
        STACKS = 2 * 3 * GROUP

        def fill(step):
            f = FILL[step]
            return f, f % 2, f // 2

        stage = [q_stack[:, :, :].rearrange("p a b -> p (a b)")[:, i * 2 * KB * FEAT:(i + 1) * 2 * KB * FEAT].bitcast(F32)
                 for i in (0, 1)]
        stage += [k_stack[:, :, :].rearrange("p a b -> p (a b)")[:, i * 2 * KB * FEAT:(i + 1) * 2 * KB * FEAT].bitcast(F32)
                  for i in (0, 1)]
        w_dram = [wl[0], wr[0], wlinT[0], wl[1], wr[1], wlinT[1], wq, wk, wv]
        W_ORDER = [2, 0, 1, 5, 3, 4, 6, 7, 8]

        block = ctx.enter_context(nc.Block())

        @block.sync
        def _(sp):
            def load_weight(i):
                if i >= 4:
                    sp.wait_ge(weight_lo, i - 3)
                sp.dma_start(stage[i % 4].rearrange("p (c n) -> p c n", c=KB),
                             w_dram[W_ORDER[i]].rearrange("(c p) n -> p c n", p=P)).then_inc(weight_loaded[i % 4], 16)

            def load_xT(n):
                need(sp, xb_done, KB * n)
                stand_alone(sp, passed_sp)
                sp.dma_start(hT[:, :, :], xT[bass.ds(n, 1)].rearrange("a (c p) s -> p (a c) s", p=P)).then_inc(xT_loaded, 16)

            def load_x(n):
                need(sp, residual_done, NB * n)
                stand_alone(sp, passed_sp)
                sp.dma_start(x_nodes[:, :, :], x[bass.ds(n, 1)].rearrange("a (b p) f -> p (a b) f", p=P)).then_inc(x_loaded, 16)

            def load_adj_layer0(n):
                need(sp, e_done, LAYERS * NB * n)
                stand_alone(sp, passed_sp)
                sp.dma_start(adjT_sb[:, :, :], adjT[bass.ds(n, 1)].rearrange("a (b p) s -> p (a b) s", p=P)).then_inc(adjT_loaded, 16)
                for j in range(NB):
                    rows = slice(j * P, (j + 1) * P)
                    sp.dma_start(edge[:, j, j * P:], adj[bass.ds(n, 1), rows, j * P:].rearrange("a p s -> p (a s)")).then_inc(edge_loaded, 16)
                    if j:
                        sp.dma_start(edge[:, j, 0:j * P], adjT[bass.ds(n, 1), rows, 0:j * P].rearrange("a p s -> p (a s)")).then_inc(edge_loaded, 16)

            def load_bias(n):
                need(sp, max_done, UNITS * n)
                stand_alone(sp, passed_sp)
                sp.dma_start(bias[:, :, :], adj[bass.ds(n, 1)].rearrange("a (b p) s -> p (a b) s", p=P)).then_inc(adj_loaded, 16)

            def store(a, i):
                sp.wait_ge(rows_done, a * NB + i + 1)
                stand_alone(sp, passed_sp)
                sp.dma_start(out[bass.ds(a, 1), i * P:(i + 1) * P, :].rearrange("a p f -> p (a f)"),
                             rows_out[:, i % 2, :]).then_inc(stored[i % 2], 16)

            def stack(n, side):
                f, b, q = fill(("W", 2, side, KB - 1))
                sp.wait_ge(emptied[b], n * BANK_FILLS + q + 1)
                stand_alone(sp, passed_sp)
                f, b, q = fill(("W", 2, side, KB - 2))
                sp.wait_ge(emptied[b], n * BANK_FILLS + q + 1)
                stand_alone(sp, passed_sp)
                parts = (hw_hi, hw_hi, hw_lo) if side == LEFT else (hw_hi, hw_lo, hw_hi)
                dst = q_stack if side == LEFT else k_stack
                for slot, part in enumerate(parts):
                    for g in range(GROUP):
                        sp.dma_start(dst[HD * slot:HD * (slot + 1), g:HEADS:GROUP, :],
                                     part[HD * g:HD * (g + 1), side, :, :]).then_inc(stacked, 16)

            def turn(n, l0, attention):
                a = n - 1
                if attention:
                    store(a, 0)
                if l0:
                    load_xT(n + 1)
                if attention:
                    store(a, 1)
                    store(a, 2)
                if l0:
                    load_adj_layer0(n + 1)
                    load_x(n + 1)
                if l0:
                    load_bias(n)
                    need(sp, pv_done, UNITS * n)
                    if attention:
                        stand_alone(sp, passed_sp)
                    stack(n, LEFT)
                if attention:
                    store(a, 3)
                if l0:
                    stack(n, RIGHT)

            load_xT(0)
            load_weight(0)
            load_weight(1)
            for dst, src in ((b_lin_rows[:, :, :], b_lin[:, :].partition_broadcast(P)),
                             (ln_a_rows[:, :], ln_a[1].partition_broadcast(P)),
                             (ln_b_rows[:, :], ln_b[1].partition_broadcast(P)),
                             (bv_rows[:, :], bv[:].partition_broadcast(P)),
                             (beta_col[:, :], beta[:].partition_broadcast(P)),
                             (ln_a_col[:, :], ln_a_by_block),
                             (ln_b_col[:, :], ln_b_by_block),
                             (qk_bias[:, 0, :], bq_by_block),
                             (qk_bias[:, 1, :], bk_by_block)):
                sp.dma_start(dst, src).then_inc(consts_loaded, 16)
            load_weight(2)
            load_adj_layer0(0)
            load_weight(3)
            load_x(0)
            for i in range(4, 9):
                load_weight(i)
            turn(0, True, False)
            with sp.Fori(1, GRAPHS) as n:
                turn(n, True, True)
            turn(GRAPHS, False, True)
            sp.wait_ge(xT_loaded, 16 * (GRAPHS + 1))
            sp.wait_ge(adjT_loaded, 16 * (GRAPHS + 1))
            sp.wait_ge(edge_loaded, 16 * (2 * NB - 1) * (GRAPHS + 1))
            sp.wait_ge(x_loaded, 16 * (GRAPHS + 1))
            sp.wait_ge(stored[0], 8 * NB * GRAPHS)
            sp.wait_ge(stored[1], 8 * NB * GRAPHS)

        @block.tensor
        def _(pe):
            def split_product(dst, lhs_hi, lhs_lo, rhs_hi, rhs_lo, ks):
                for k in ks:
                    for j, (a, b) in enumerate(((lhs_hi, rhs_hi), (lhs_hi, rhs_lo), (lhs_lo, rhs_hi))):
                        last = nc.tensor.matmul(dst, a(k), b(k), start=(k == ks[0] and j == 0),
                                                stop=(k == ks[-1] and j == 2))
                return last

            def bank_free(n, b, q):
                need(pe, emptied[b], n * BANK_FILLS + q)

            def emptied_all(n, step):
                f, b, q = fill(step)
                pe.wait_ge(emptied[b], n * BANK_FILLS + q + 1)
                pe.wait_ge(emptied[1 - b], n * BANK_FILLS + (f - 1) // 2 + 1)

            def layer_input(l):
                return (xa_hi, xa_lo) if l == 0 else (xb_hi, xb_lo)

            def lin(n, l, j):
                f, b, q = fill(("lin", l, j))
                if j == 0:
                    if l == 0:
                        pe.wait_ge(xa_done, n + 1)
                        if isinstance(n, int) and n == 0:
                            pe.wait_ge(weight_lo, 1)
                    else:
                        pe.wait_ge(xb_done, KB * (n + 1))
                        if isinstance(n, int) and n == 0:
                            pe.wait_ge(weight_lo, 4)
                hi, lo = layer_input(l)
                bank_free(n, b, q)
                rows = slice(j * P, (j + 1) * P)
                w = 3 * l + LIN
                split_product(work[b][:, 0:FEAT], lambda k: hi[:, k, rows], lambda k: lo[:, k, rows],
                              lambda k: w_hi[:, w, k, :], lambda k: w_lo[:, w, k, :],
                              range(KB)).then_inc(work_ready, 1)

            def W(n, l, side, m):
                f, b, q = fill(("W", l, side, m))
                if l == 2 and side == LEFT and m == 0:
                    emptied_all(n, ("T", 1, KB - 1))
                if isinstance(n, int) and n == 0 and m == 0:
                    pe.wait_ge(weight_lo, (2, 3, 5, 6, 7, 8)[2 * l + side])
                hi, lo = layer_input(l)
                bank_free(n, b, q)
                w = 3 * l + side
                cols = slice(m * P, (m + 1) * P)
                split_product(work[b][:, :], lambda k: w_hi[:, w, k, cols], lambda k: w_lo[:, w, k, cols],
                              lambda k: hi[:, k, :], lambda k: lo[:, k, :],
                              range(KB)).then_inc(work_ready, 1)

            def u(n, l, j):
                f, b, q = fill(("u", l, j))
                if j == 0:
                    emptied_all(n, ("W", l, RIGHT, KB - 1))
                hi, lo = layer_input(l)
                rows = slice(j * P, (j + 1) * P)
                for side, cols in ((LEFT, slice(0, (j + 1) * P)), (RIGHT, slice(j * P, NODES))):
                    bb, qq = (f + side) % 2, (f + side) // 2
                    bank_free(n, bb, qq)
                    split_product(work[bb][:, cols], lambda k: hi[:, k, rows], lambda k: lo[:, k, rows],
                                  lambda k: hw_hi[:, side, k, cols], lambda k: hw_lo[:, side, k, cols],
                                  range(KB)).then_inc(work_ready, 1)

            def ctx_rows(n, l, i):
                f, b, q = fill(("ctx", l, i))
                if i == 0:
                    pe.wait_ge(hl_lo_done, n * LAYERS * NB + (l + 1) * NB)
                    pe.wait_ge(e_lo_done, n * LAYERS * NB + (l + 1) * NB)
                bank_free(n, b, q)
                cols = slice(i * P, (i + 1) * P)
                for j in range(NB):
                    nc.tensor.matmul(work[b][:, 0:FEAT + 2], e_hi[:, j, cols], hl_hi[:, j, :], start=(j == 0), stop=False)
                    nc.tensor.matmul(work[b][:, 0:FEAT], e_hi[:, j, cols], hl_lo[:, j, :], start=False, stop=False)
                    last = nc.tensor.matmul(work[b][:, 0:FEAT + 2], e_lo[:, j, cols], hl_hi[:, j, :], start=False,
                                            stop=(j == NB - 1))
                last.then_inc(work_ready, 1)

            def transpose_rows(n, l, k):
                f, b, q = fill(("T", l, k))
                if k == 0:
                    pe.wait_ge(normed, n * LAYERS * NB + (l + 1) * NB)
                    if isinstance(n, int) and n == 0 and l == 0:
                        pe.wait_ge(pool_consts, 2)
                bank_free(n, b, q)
                for i in range(NB):
                    last = nc.tensor.transpose(work[b][:, i * P:(i + 1) * P], nat[:, i, k * P:(k + 1) * P], ident[:, :])
                last.then_inc(work_ready, 1)

            def v(n, j):
                f, b, q = fill(("v", j))
                if isinstance(n, int) and n == 0 and j == 0:
                    pe.wait_ge(weight_lo, 9)
                bank_free(n, b, q)
                rows = slice(j * P, (j + 1) * P)
                split_product(work[b][:, 0:FEAT], lambda k: xb_hi[:, k, rows], lambda k: xb_lo[:, k, rows],
                              lambda k: w_hi[:, W_V, k, :], lambda k: w_lo[:, W_V, k, :],
                              range(KB)).then_inc(work_ready, 1)

            def qk(a, s):
                i, h = divmod(s, HEADS)
                if s == 0:
                    pe.wait_ge(stacked, 16 * STACKS * (a + 1))
                else:
                    if s >= 2:
                        pe.wait_ge(max_done, a * UNITS + s - 1)
                nc.tensor.matmul(scores[s % 2][:, :], q_stack[0:3 * HD, h, i * P:(i + 1) * P], k_stack[0:3 * HD, h, :],
                                 start=True, stop=True).then_inc(qk_done, 1)

            def transpose_probs(a, s):
                pe.wait_ge(probs_done, a * UNITS + s + 1)
                if s >= 2:
                    pe.wait_ge(pT_lo_done, a * UNITS + s - 1)
                for j in range(NB):
                    last = nc.tensor.transpose(probsT[s % 2][:, j * P:(j + 1) * P], probs[:, s % DEPTH, j * P:(j + 1) * P],
                                               ident[:, :])
                last.then_inc(probsT_done, 1)

            def pv(a, s):
                i, h = divmod(s, HEADS)
                b, c = divmod(h, HALF)
                pe.wait_ge(pT_lo_done, a * UNITS + s + 1)
                if s == 0:
                    pe.wait_ge(emptied[0], BANK_FILLS * (a + 1))
                    pe.wait_ge(emptied[1], BANK_FILLS * (a + 1))
                if c == 0:
                    need(pe, reduced, a * 2 * NB + (2 * (i - 1) + b + 1 if i else 0))
                cols = slice(c * 2 * HD, (c + 1) * 2 * HD)
                high = slice(c * 2 * HD, c * 2 * HD + HD)
                for j in range(NB):
                    nodes = slice(j * P, (j + 1) * P)
                    nc.tensor.matmul(heads_out[b][:, cols], pT_hi[:, s % DEPTH, nodes], v_sb[:, j, h, :],
                                     start=(j == 0), stop=False)
                    last = nc.tensor.matmul(heads_out[b][:, high], pT_lo[:, s % DEPTH, nodes], v_sb[:, j, h, 0:HD],
                                            start=False, stop=(j == NB - 1))
                last.then_inc(pv_done, 1)

            def turn(n, l0, attention):
                a = n - 1
                for step in schedule(l0, attention):
                    kind, at = step[0], step[1:]
                    if kind == "lin":
                        lin(n, *at)
                    elif kind == "W":
                        W(n, *at)
                    elif kind == "u":
                        u(n, *at)
                    elif kind == "ctx":
                        ctx_rows(n, *at)
                    elif kind == "T":
                        transpose_rows(n, *at)
                    elif kind == "v":
                        v(n, *at)
                    elif kind == "qk":
                        qk(a, *at)
                    elif kind == "t":
                        transpose_probs(a, *at)
                    elif kind == "pv":
                        pv(a, *at)

            turn(0, True, False)
            with pe.Fori(1, GRAPHS) as n:
                turn(n, True, True)
            turn(GRAPHS, False, True)

        @block.scalar
        def _(act):
            def split_x(n):
                act.wait_ge(xT_loaded, 16 * (n + 1))
                nc.scalar.copy(xa_hi[:, :, :], hT[:, :, :]).then_inc(xa_hi_done, 1)

            def fill_high(n, step, dst, b, f, bias_=None, src=None):
                act.wait_ge(work_ready, n * FILLS + f + 1)
                src = work[b][:, :] if src is None else src
                if bias_ is None:
                    nc.scalar.copy(dst, src).then_inc(hi_done, 1)
                else:
                    nc.scalar.activation(dst, src, ACT.Identity, bias=bias_).then_inc(hi_done, 1)

            def W(n, l, side, m):
                f, b, q = fill(("W", l, side, m))
                if l == 0 and side == LEFT and m == 0:
                    need(act, stacked, 16 * STACKS * n)
                fill_high(n, None, hw_hi[:, side, m, :], b, f, qk_bias[:, side, m:m + 1] if l == 2 else None)

            def lin(n, l, j):
                f, b, q = fill(("lin", l, j))
                act.wait_ge(emptied[b], n * BANK_FILLS + q + 1)
                nc.scalar.copy(hl_hi[:, j, 0:FEAT], nat[:, j, 0:FEAT]).then_inc(hl_hi_done, 1)

            def exp_row(n, l, j):
                act.wait_ge(z_done, n * LAYERS * NB + l * NB + j + 1)
                nc.scalar.activation(erow[:, j % 3, :], erow[:, j % 3, :], ACT.Exp).then_inc(exp_done, 1)

            def e_high(n, l, j):
                act.wait_ge(e_done, n * LAYERS * NB + l * NB + j + 1)
                nc.scalar.copy(e_hi[:, j, :], erow[:, j % 3, :]).then_inc(e_hi_done, 1)

            def ctx_rows(n, l, i):
                f, b, q = fill(("ctx", l, i))
                act.wait_ge(work_ready, n * FILLS + f + 1)
                nc.scalar.copy(nat[:, i, :], work[b][:, 0:FEAT + 2]).then_inc(emptied[b], 1)

            def transposed(n, l, k):
                f, b, q = fill(("T", l, k))
                if l == 0:
                    act.wait_ge(work_ready, n * FILLS + f + 1)
                    nc.scalar.activation(hT[:, k, :], work[b][:, :], ACT.Relu, bias=ln_b_col[:, k:k + 1],
                                         scale=ln_a_col[:, k:k + 1]).then_inc(emptied[b], 1)
                else:
                    fill_high(n, None, xb_hi[:, k, :], b, f)

            def v(n, j):
                f, b, q = fill(("v", j))
                fill_high(n, None, v_sb[:, j, :, 0:HD], b, f,
                          src=work[b][:, 0:FEAT].rearrange("p (h d) -> p h d", d=HD))

            def exp_scores(a, s):
                act.wait_ge(max_done, a * UNITS + s + 1)
                if s >= DEPTH:
                    act.wait_ge(probsT_done, a * UNITS + s - DEPTH + 1)
                nc.scalar.activation(probs[:, s % DEPTH, :], neg_scores[:, s % 2, :], ACT.Exp, bias=neg_max[:, s:s + 1],
                                     scale=-1.0, accum_out=row_sum[:, s:s + 1]).then_inc(probs_done, 1)

            def pT_high(a, s):
                act.wait_ge(probsT_done, a * UNITS + s + 1)
                if s >= DEPTH:
                    act.wait_ge(pv_done, a * UNITS + s - DEPTH + 1)
                nc.scalar.mul(pT_hi[:, s % DEPTH, :], probsT[s % 2][:, :], P_SCALE).then_inc(pT_hi_done, 1)

            def turn(n, l0, attention):
                a = n - 1
                for step in schedule(l0, attention):
                    kind, at = step[0], step[1:]
                    if kind == "next_x":
                        split_x(n + 1)
                    elif kind == "W":
                        W(n, *at)
                    elif step[0:2] == ("after", "lin"):
                        lin(n, *step[2:])
                    elif step[0:2] == ("after", "u"):
                        exp_row(n, *step[2:])
                    elif kind == "E":
                        e_high(n, *at)
                    elif kind == "ctx":
                        ctx_rows(n, *at)
                    elif kind == "T":
                        transposed(n, *at)
                    elif kind == "v":
                        v(n, *at)
                    elif kind == "exp":
                        exp_scores(a, *at)
                    elif kind == "t":
                        pT_high(a, *at)

            split_x(0)
            for i in range(9):
                act.wait_ge(weight_loaded[i % 4], 16 * (i // 4 + 1))
                nc.scalar.mul(w_hi[:, W_ORDER[i], :, :].rearrange("p c n -> p (c n)"), stage[i % 4],
                              W_SCALE).then_inc(weight_hi, 1)
                if i == 0:
                    act.wait_ge(consts_scaled, 1)
            turn(0, True, False)
            with act.Fori(1, GRAPHS) as n:
                turn(n, True, True)
            turn(GRAPHS, False, True)

        @block.vector
        def _(dve):
            def make_bias(n, i):
                if i == 0:
                    dve.wait_ge(adj_loaded, 16 * (n + 1))
                    need(dve, probs_done, UNITS * n)
                need(dve, bias_done, n * NB + i)
                nc.vector.tensor_scalar(masked, bias[:, i, :], 0.0, MASKED * SCORE_SCALE, ALU.is_le,
                                        ALU.mult).then_inc(masked_done, 1)
                dve.wait_ge(masked_done, n * NB + i + 1)
                nc.vector.scalar_tensor_tensor(out=bias[:, i, :], in0=bias[:, i, :], scalar=beta_col[:, 0:1],
                                               in1=masked, op0=ALU.mult, op1=ALU.add).then_inc(bias_done, 1)

            def hi_index(step):
                return HI_FILLS.index(step)

            def W(n, l, side, m):
                step = ("W", l, side, m)
                f, b, q = fill(step)
                dve.wait_ge(hi_done, n * HIS + hi_index(step) + 1)
                if l < 2:
                    nc.vector.tensor_sub(hw_lo[:, side, m, :], work[b][:, :], hw_hi[:, side, m, :]).then_inc(emptied[b], 1)
                else:
                    nc.vector.scalar_tensor_tensor(out=hw_lo[:, side, m, :], in0=work[b][:, :],
                                                   scalar=qk_bias[:, side, m:m + 1], in1=hw_hi[:, side, m, :],
                                                   op0=ALU.add, op1=ALU.subtract).then_inc(emptied[b], 1)

            def lin(n, l, j):
                f, b, q = fill(("lin", l, j))
                if l == 0 and j == 0:
                    need(dve, x2_bv_done, NB * n)
                dve.wait_ge(work_ready, n * FILLS + f + 1)
                nc.vector.scalar_tensor_tensor(out=nat[:, j, 0:FEAT], in0=work[b][:, 0:FEAT], scalar=1.0 / W_SCALE,
                                               in1=b_lin_rows[:, l, :], op0=ALU.mult, op1=ALU.add).then_inc(emptied[b], 1)

            def exponents(n, l, j):
                f = FILL[("u", l, j)]
                left, right = f % 2, (f + 1) % 2
                c = 1.0 / (W_SCALE * TEMPER)
                if l == 0 and j == 0:
                    dve.wait_ge(selected, n + 1)
                need(dve, z_done, n * LAYERS * NB + l * NB + j)
                need(dve, e_lo_done, n * LAYERS * NB + l * NB + max(j - 2, 0))
                dve.wait_ge(work_ready, n * FILLS + f + 1)
                if j:
                    nc.vector.scalar_tensor_tensor(out=erow[:, j % 3, 0:j * P], in0=work[left][:, 0:j * P], scalar=c,
                                                   in1=edge[:, j, 0:j * P], op0=ALU.mult, op1=ALU.mult)
                nc.vector.scalar_tensor_tensor(out=diag_part[:, :], in0=work[left][:, j * P:(j + 1) * P], scalar=c,
                                               in1=edge_diag[:, j, :], op0=ALU.mult, op1=ALU.mult).then_inc(emptied[left], 1)
                dve.wait_ge(work_ready, n * FILLS + f + 2)
                nc.vector.scalar_tensor_tensor(out=erow[:, j % 3, j * P:], in0=work[right][:, j * P:], scalar=c,
                                               in1=edge[:, j, j * P:], op0=ALU.mult, op1=ALU.mult).then_inc(emptied[right], 1)
                dve.wait_ge(emptied[right], n * BANK_FILLS + (f + 1) // 2 + 1)
                nc.vector.tensor_add(erow[:, j % 3, j * P:(j + 1) * P], erow[:, j % 3, j * P:(j + 1) * P],
                                     diag_part[:, :]).then_inc(z_done, 1)

            def ctx_rows(n, l, i):
                f, b, q = fill(("ctx", l, i))
                dve.wait_ge(emptied[b], n * BANK_FILLS + q + 1)
                nc.vector.bn_stats(stats[:, i, :], nat[:, i, 0:FEAT]).then_inc(stats_done, 1)

            def moments_of_ctx(n, l):
                per = n * LAYERS + l
                dve.wait_ge(stats_done, n * LAYERS * NB + (l + 1) * NB)
                stand_alone(dve, passed_dve)
                for i in range(NB):
                    last = nc.vector.bn_aggr(moments[:, i, :], stats[:, i, :])
                last.then_inc(moments_done, 1)
                nc.vector.tensor_scalar(eps_sum[:, :], nat[:, :, FEAT], 1e-10, 1e-3, ALU.add, ALU.mult)
                dve.wait_ge(moments_done, per + 1)
                nc.vector.tensor_scalar(var_floor[:, :], moments[:, :, 1], 1e-36, None, ALU.max).then_inc(floor_done, 1)

            def norm(n, l):
                per = n * LAYERS + l
                dve.wait_ge(deviation_done, per + 1)
                nc.vector.scalar_tensor_tensor(out=denom[:, :], in0=deviation[:, :],
                                               scalar=float(np.sqrt(FEAT / (FEAT - 1.0))), in1=eps_sum[:, :],
                                               op0=ALU.mult, op1=ALU.add).then_inc(denom_done, 1)
                dve.wait_ge(denom_done, per + 1)
                nc.vector.reciprocal(factor[:, :], denom[:, :]).then_inc(factor_done, 1)
                dve.wait_ge(factor_done, per + 1)
                for i in range(NB):
                    nc.vector.tensor_scalar(nat[:, i, 0:FEAT], nat[:, i, 0:FEAT], moments[:, i, 0:1],
                                            factor[:, i:i + 1], ALU.subtract, ALU.mult).then_inc(normed if l == 0 else scaled, 1)

            def relu(n, i):
                if i == 0:
                    dve.wait_ge(x_loaded, 16 * (n + 1))
                dve.wait_ge(affine_done, n * NB + i + 1)
                nc.vector.scalar_tensor_tensor(out=nat[:, i, 0:FEAT], in0=nat[:, i, 0:FEAT], scalar=0.0,
                                               in1=x_nodes[:, i, :], op0=ALU.max, op1=ALU.add).then_inc(residual_done, 1)
                dve.wait_ge(residual_done, n * NB + i + 1)
                nc.vector.bn_stats(stats2[:, i, :], nat[:, i, 0:FEAT]).then_inc(stats2_done, 1)

            def moments2_of_rows(n):
                dve.wait_ge(stats2_done, (n + 1) * NB)
                stand_alone(dve, passed_dve)
                for i in range(NB):
                    last = nc.vector.bn_aggr(moments2[:, i, :], stats2[:, i, :])
                last.then_inc(moments2_done, 1)

            def norm2(n):
                dve.wait_ge(factor2_done, n + 1)
                for i in range(NB):
                    nc.vector.tensor_scalar(nat[:, i, 0:FEAT], nat[:, i, 0:FEAT], moments2[:, i, 0:1],
                                            factor2[:, i:i + 1], ALU.subtract, ALU.mult).then_inc(normed, 1)

            def transposed(n, l, k):
                step = ("T", l, k)
                f, b, q = fill(step)
                if l == 0:
                    dve.wait_ge(emptied[b], n * BANK_FILLS + q + 1)
                    nc.vector.tensor_copy(xb_hi[:, k, :], hT[:, k, :]).then_inc(xb_hi_done, 1)
                    dve.wait_ge(xb_hi_done, n * KB + k + 1)
                    nc.vector.tensor_sub(xb_lo[:, k, :], hT[:, k, :], xb_hi[:, k, :]).then_inc(xb_done, 1)
                else:
                    dve.wait_ge(hi_done, n * HIS + hi_index(step) + 1)
                    nc.vector.tensor_sub(xb_lo[:, k, :], work[b][:, :], xb_hi[:, k, :]).then_inc(emptied[b], 1)

            def v(n, j):
                step = ("v", j)
                f, b, q = fill(step)
                dve.wait_ge(hi_done, n * HIS + hi_index(step) + 1)
                nc.vector.tensor_sub(v_sb[:, j, :, HD:2 * HD], work[b][:, 0:FEAT].rearrange("p (h d) -> p h d", d=HD),
                                     v_sb[:, j, :, 0:HD]).then_inc(emptied[b], 1)

            def masked_scores(a, s):
                i, h = divmod(s, HEADS)
                if s == 0:
                    dve.wait_ge(bias_done, NB * (a + 1))
                dve.wait_ge(qk_done, a * UNITS + s + 1)
                if s >= 2:
                    dve.wait_ge(probs_done, a * UNITS + s - 1)
                stand_alone(dve, passed_dve)
                nc.vector.tensor_tensor_reduce(out=neg_scores[:, s % 2, :], in0=scores[s % 2][:, :], in1=bias[:, i, :],
                                               scale=-1.0 / SCORE_SCALE, scalar=3.0e38, op0=ALU.add, op1=ALU.min,
                                               accum_out=neg_max[:, s:s + 1]).then_inc(max_done, 1)

            def pT_low(a, s):
                dve.wait_ge(pT_hi_done, a * UNITS + s + 1)
                nc.vector.scalar_tensor_tensor(out=pT_lo[:, s % DEPTH, :], in0=probsT[s % 2][:, :], scalar=P_SCALE,
                                               in1=pT_hi[:, s % DEPTH, :], op0=ALU.mult, op1=ALU.subtract).then_inc(pT_lo_done, 1)

            def reduce(a, i, b):
                dve.wait_ge(pv_done, a * UNITS + HEADS * i + HALF * (b + 1))
                dve.wait_ge(stored[i % 2], 16 * (a * (NB // 2) + i // 2))
                nc.vector.tensor_reduce(
                    rows_out[:, i % 2, b * HALF * HD:(b + 1) * HALF * HD].rearrange("p (h d) -> p h d", d=HD),
                    heads_out[b][:, 0:HALF * 2 * HD].rearrange("p (h e d) -> p h d e", e=2, d=HD),
                    axis=AX.X, op=ALU.add).then_inc(reduced, 1)

            def merge(a, i):
                dve.wait_ge(probs_done, a * UNITS + HEADS * (i + 1))
                need(dve, rows_scaled, a * NB + i)
                nc.vector.tensor_scalar(scaled_sum[:, :], row_sum[:, HEADS * i:HEADS * (i + 1)], W_SCALE * P_SCALE, None,
                                        ALU.mult).then_inc(sum_scaled, 1)
                dve.wait_ge(sum_scaled, a * NB + i + 1)
                nc.vector.reciprocal(inv_sum[:, :], scaled_sum[:, :]).then_inc(sum_inverted, 1)

            def moments_of_rows(a, i):
                dve.wait_ge(rows_merged, a * NB + i + 1)
                need(dve, rows_done, a * NB + i)
                nc.vector.bn_stats(stats3[:, :], rows_out[:, i % 2, :]).then_inc(stats3_done, 1)
                dve.wait_ge(stats3_done, a * NB + i + 1)
                stand_alone(dve, passed_dve)
                nc.vector.bn_aggr(moments3[:, :], stats3[:, :]).then_inc(moments3_done, 1)

            def finish(a, i):
                dve.wait_ge(factor3_done, a * NB + i + 1)
                nc.vector.tensor_scalar(rows_out[:, i % 2, :], rows_out[:, i % 2, :], moments3[:, 0:1], factor3[:, 0:1],
                                        ALU.subtract, ALU.mult).then_inc(rows_done, 1)

            def turn(n, l0, attention):
                a = n - 1
                for step in schedule(l0, attention):
                    kind, at = step[0], step[1:]
                    if step[0:2] == ("after", "W"):
                        W(n, *step[2:])
                    elif kind == "lin":
                        lin(n, *at)
                    elif kind == "u":
                        exponents(n, *at)
                    elif step[0:2] == ("after", "ctx"):
                        ctx_rows(n, *step[2:])
                    elif kind == "moments0":
                        moments_of_ctx(n, *at)
                    elif kind == "norm":
                        norm(n, *at)
                    elif kind == "relu":
                        relu(n, *at)
                    elif kind == "moments2":
                        moments2_of_rows(n)
                    elif kind == "norm2":
                        norm2(n)
                    elif step[0:2] == ("after", "T"):
                        transposed(n, *step[2:])
                    elif kind == "bias":
                        make_bias(n, *at)
                    elif step[0:2] == ("after", "v"):
                        v(n, *step[2:])
                    elif kind == "qk":
                        masked_scores(a, *at)
                    elif kind == "low_t":
                        pT_low(a, *at)
                    elif kind == "reduce":
                        reduce(a, *at)
                    elif kind == "merge":
                        merge(a, *at)
                    elif kind == "moments":
                        moments_of_rows(a, *at)
                    elif kind == "finish":
                        finish(a, *at)

            nc.vector.memset(hl_hi[:, :, FEAT:FEAT + 2].bitcast(F32), 1.0)
            dve.wait_ge(consts_loaded, 16 * 9)
            nc.vector.tensor_scalar(beta_col[:, :], beta_col[:, :], SCORE_SCALE, None, ALU.mult)
            nc.vector.tensor_scalar(qk_bias[:, :, :], qk_bias[:, :, :], W_SCALE, None, ALU.mult).then_inc(consts_scaled, 1)
            for i in range(9):
                dve.wait_ge(weight_hi, i + 1)
                nc.vector.scalar_tensor_tensor(out=w_lo[:, W_ORDER[i], :, :].rearrange("p c n -> p (c n)"), in0=stage[i % 4],
                                               scalar=W_SCALE, in1=w_hi[:, W_ORDER[i], :, :].rearrange("p c n -> p (c n)"),
                                               op0=ALU.mult, op1=ALU.subtract).then_inc(weight_lo, 1)
            dve.wait_ge(consts_scaled, 1)
            turn(0, True, False)
            with dve.Fori(1, GRAPHS) as n:
                turn(n, True, True)
            turn(GRAPHS, False, True)

        @block.gpsimd
        def _(pool):
            def split_x(n):
                pool.wait_ge(xa_hi_done, n + 1)
                nc.gpsimd.tensor_sub(xa_lo[:, :, :], hT[:, :, :], xa_hi[:, :, :]).then_inc(xa_done, 1)

            def select(n):
                pool.wait_ge(adjT_loaded, 16 * (n + 1))
                pool.wait_ge(edge_loaded, 16 * (2 * NB - 1) * (n + 1))
                stand_alone(pool, passed_pool)
                for j in range(NB):
                    cols = slice(j * P, (j + 1) * P)
                    nc.gpsimd.affine_select(out=edge_diag[:, j, :], in_=adjT_sb[:, j, cols], compare_op=ALU.is_ge,
                                            fill=0.0, base=0, pattern=[[-1, P]], channel_multiplier=1)
                    last = nc.gpsimd.affine_select(out=edge[:, j, cols], in_=edge[:, j, cols], compare_op=ALU.is_gt,
                                                   fill=0.0, base=0, pattern=[[1, P]], channel_multiplier=-1)
                last.then_inc(selected, 1)

            def e_low(n, l, j):
                pool.wait_ge(e_hi_done, n * LAYERS * NB + l * NB + j + 1)
                nc.gpsimd.tensor_sub(e_lo[:, j, :], erow[:, j % 3, :], e_hi[:, j, :].bitcast(F32)).then_inc(e_lo_done, 1)

            def hl_low(n, l, j):
                pool.wait_ge(hl_hi_done, n * LAYERS * NB + l * NB + j + 1)
                nc.gpsimd.tensor_sub(hl_lo[:, j, :], nat[:, j, 0:FEAT], hl_hi[:, j, 0:FEAT].bitcast(F32)).then_inc(hl_lo_done, 1)

            def times_adj(n, l, j):
                pool.wait_ge(exp_done, n * LAYERS * NB + l * NB + j + 1)
                nc.gpsimd.tensor_mul(erow[:, j % 3, :], erow[:, j % 3, :], adjT_sb[:, j, :]).then_inc(e_done, 1)

            def deviation_of_ctx(n, l):
                pool.wait_ge(floor_done, n * LAYERS + l + 1)
                nc.gpsimd.tensor_tensor(deviation[:, :], var_floor[:, :], half[:, :], ALU.pow).then_inc(deviation_done, 1)

            def affine(n, i):
                pool.wait_ge(scaled, n * NB + i + 1)
                nc.gpsimd.tensor_mul(nat[:, i, 0:FEAT], nat[:, i, 0:FEAT], ln_a_rows[:, :]).then_inc(times_a, 1)
                pool.wait_ge(times_a, n * NB + i + 1)
                nc.gpsimd.tensor_add(nat[:, i, 0:FEAT], nat[:, i, 0:FEAT], ln_b_rows[:, :]).then_inc(affine_done, 1)

            def factor_of_x2(n):
                pool.wait_ge(moments2_done, n + 1)
                nc.gpsimd.tensor_add(var2[:, :], moments2[:, :, 1], norm_eps[:, :]).then_inc(var2_done, 1)
                pool.wait_ge(var2_done, n + 1)
                nc.gpsimd.tensor_tensor(factor2[:, :], var2[:, :], minus_half[:, :], ALU.pow).then_inc(factor2_done, 1)

            def residual(n):
                pool.wait_ge(normed, n * LAYERS * NB + 2 * NB)
                for i in range(NB):
                    nc.gpsimd.tensor_add(x2_bv[:, i, :], nat[:, i, 0:FEAT], bv_rows[:, :]).then_inc(x2_bv_done, 1)

            def merge(a, i):
                pool.wait_ge(sum_inverted, a * NB + i + 1)
                pool.wait_ge(reduced, a * 2 * NB + 2 * i + 2)
                rows = rows_out[:, i % 2, :].rearrange("p (h d) -> p h d", d=HD)
                nc.gpsimd.tensor_tensor(rows, rows, inv_sum[:, :].unsqueeze(2).to_broadcast([P, HEADS, HD]),
                                        ALU.mult).then_inc(rows_scaled, 1)
                pool.wait_ge(rows_scaled, a * NB + i + 1)
                nc.gpsimd.tensor_add(rows_out[:, i % 2, :], rows_out[:, i % 2, :], x2_bv[:, i, :]).then_inc(rows_merged, 1)

            def factor_of_rows(a, i):
                pool.wait_ge(moments3_done, a * NB + i + 1)
                nc.gpsimd.tensor_add(var3[:, :], moments3[:, 1:2], norm_eps[:, 0:1]).then_inc(var3_done, 1)
                pool.wait_ge(var3_done, a * NB + i + 1)
                nc.gpsimd.tensor_tensor(factor3[:, :], var3[:, :], minus_half[:, 0:1], ALU.pow).then_inc(factor3_done, 1)

            def turn(n, l0, attention):
                a = n - 1
                for step in schedule(l0, attention):
                    kind, at = step[0], step[1:]
                    if kind == "next_x":
                        split_x(n + 1)
                    elif kind == "E":
                        e_low(n, *at)
                    elif kind == "select":
                        residual(n)
                        select(n + 1)
                    elif step[0:2] == ("after", "lin"):
                        hl_low(n, *step[2:])
                    elif step[0:2] == ("after", "u"):
                        times_adj(n, *step[2:])
                    elif kind == "moments0":
                        deviation_of_ctx(n, *at)
                    elif kind == "relu":
                        affine(n, *at)
                    elif kind == "moments2":
                        factor_of_x2(n)
                    elif kind == "merge":
                        merge(a, *at)
                    elif kind == "moments":
                        factor_of_rows(a, *at)

            nc.gpsimd.memset(half[:, :], 0.5)
            nc.gpsimd.memset(minus_half[:, :], -0.5)
            nc.gpsimd.memset(norm_eps[:, :], 1e-5)
            nc.gpsimd.memset(ident[:, :], 0.0).then_inc(pool_consts, 1)
            pool.wait_ge(pool_consts, 1)
            nc.gpsimd.affine_select(out=ident[:, :], in_=ident[:, :], compare_op=ALU.not_equal, fill=1.0, base=0,
                                    pattern=[[-1, P]], channel_multiplier=1).then_inc(pool_consts, 1)
            split_x(0)
            pool.wait_ge(consts_scaled, 1)
            select(0)
            turn(0, True, False)
            with pool.Fori(1, GRAPHS) as n:
                turn(n, True, True)
            turn(GRAPHS, False, True)


def kernel(**inputs):
    import concourse.bacc as bacc
    from concourse.bass_utils import run_bass_kernel_spmd

    def one_more(a):
        return np.concatenate([a, a[:1]])

    def by_block(a):
        return np.asarray(a).reshape(KB, P).T

    x = np.asarray(inputs["x"])
    adj = np.asarray(inputs["adj"])
    arrays = {
        "x": one_more(x),
        "xT": one_more(x.transpose(0, 2, 1)),
        "adj": one_more(adj),
        "adjT": one_more(adj.transpose(0, 2, 1)),
        "wl": inputs["L0_gnn_W_left"],
        "wr": inputs["L0_gnn_W_right"],
        "wlinT": np.asarray(inputs["L0_gnn_W_lin"]).transpose(0, 2, 1),
        "b_lin": inputs["L0_gnn_b_lin"],
        "ln_a": inputs["L0_gnn_ln_a"],
        "ln_b": inputs["L0_gnn_ln_b"],
        "ln_a_by_block": by_block(inputs["L0_gnn_ln_a"][0]),
        "ln_b_by_block": by_block(inputs["L0_gnn_ln_b"][0]),
        "wq": inputs["L1_gnn_Wq"],
        "bq_by_block": by_block(inputs["L1_gnn_bq"]),
        "wk": inputs["L1_gnn_Wk"],
        "bk_by_block": by_block(inputs["L1_gnn_bk"]),
        "wv": inputs["L1_gnn_Wv"],
        "bv": inputs["L1_gnn_bv"],
        "beta": np.asarray(inputs["L1_gnn_beta"]).reshape(1),
    }
    arrays = {f"in_{k}": np.ascontiguousarray(v) for k, v in arrays.items()}
    nc = bacc.Bacc("TRN2", target_bir_lowering=False, num_devices=1)
    args = [nc.dram_tensor(k, v.shape, mybir.dt.from_np(v.dtype), kind="ExternalInput").ap() for k, v in arrays.items()]
    out = nc.dram_tensor("out_0", (GRAPHS, NODES, FEAT), F32, kind="ExternalOutput").ap()
    graph_layers(nc, *args, out)
    r = run_bass_kernel_spmd(nc, [arrays], core_ids=[0])
    return r.results[0]["out_0"]
```

```python
from contextlib import ExitStack

import numpy as np

import concourse.bass as bass
from concourse import mybir

ALU = mybir.AluOpType
ACT = mybir.ActivationFunctionType
AX = mybir.AxisListType
F32 = mybir.dt.float32
F32R = mybir.dt.float32r
F16 = mybir.dt.float16

P = 128
GRAPHS, NODES, FEAT = 16, 512, 384
NB = NODES // P
KB = FEAT // P
LAYERS = 2
HEADS = 12
HD = FEAT // HEADS
GROUP = P // HD
UNITS = NB * HEADS
HALF = HEADS // 2

W_SCALE = 64.0
P_SCALE = 1024.0
TEMPER = float(np.sqrt(FEAT))
SCORE_SCALE = W_SCALE * W_SCALE * float(np.sqrt(HD))
MASKED = -9000000000000000.0
LEFT, RIGHT, LIN = 0, 1, 2
W_Q, W_K, W_V = 6, 7, 8


def l0_steps():
    steps = []
    for j in range(NB):
        steps += [("lin", 0, j), ("bias", j)]
    for l in range(LAYERS):
        if l:
            steps += [("lin", l, 0), ("lin", l, 1)]
        steps += [("W", l, side, m) for side in (LEFT, RIGHT) for m in range(KB)]
        if l:
            steps += [("lin", l, 2)]
        steps += [("u", l, 0), ("u", l, 1), ("u", l, 2)]
        if l:
            steps += [("lin", l, 3)]
        steps += [("E", l, 0), ("u", l, 3), ("E", l, 1), ("E", l, 2), ("E", l, 3)]
        steps += [("ctx", l, i) for i in range(NB)] + [("moments0", l), ("norm", l)]
        if l:
            steps += [("relu", i) for i in range(NB)] + [("moments2",), ("norm2",)]
        steps += [("T", l, k) for k in range(KB)]
    steps += [("next_x",)] + [("W", 2, side, m) for side in (LEFT, RIGHT) for m in range(KB)]
    steps += [("residual",)] + [("v", j) for j in range(NB)]
    return steps


def attention_steps():
    beats = []
    for s in range(UNITS + V_LAG + 4):
        for kinds in ((("qk", 0), ("exp", 1)), (("t", T_LAG), ("low_t", T_LAG + 1)), (("pv", V_LAG),)):
            beats.append([(kind, s - lag) for kind, lag in kinds if lag <= s < UNITS + lag])
        for i in range(NB):
            ends = HEADS * (i + 1) + V_LAG
            if s == ends - HALF:
                beats[-1].append(("reduce", i, 0))
            if s == ends:
                beats[-1] += [("reduce", i, 1), ("merge", i)]
            if s == ends + 2:
                beats[-1].append(("moments", i))
            if s == ends + 3:
                beats[-1].append(("finish", i))
    return beats


BEATS_AHEAD = [
    (0, 0, 0, 0), (0, 0, 0, 0), (0, 0, 0, 0), (0, 0, 0, 0),
    (0, 0, 0, 0), (0, 1, 0, 0), (0, 1, 0, 0), (0, 1, 0, 2),
    (0, 1, 0, 5), (0, 1, 0, 15), (4, 1, 1, 15), (6, 1, 2, 15),
    (6, 1, 5, 15), (8, 7, 8, 15), (14, 15, 13, 15), (14, 16, 15, 15),
    (17, 19, 17, 16), (20, 19, 20, 16), (20, 23, 21, 16), (20, 25, 21, 16),
    (20, 29, 26, 16), (32, 31, 44, 16), (37, 37, 44, 22), (43, 42, 50, 23),
    (49, 48, 51, 23), (52, 51, 54, 23), (61, 51, 54, 23), (61, 59, 56, 23),
    (64, 62, 65, 34), (64, 62, 65, 34), (67, 62, 66, 66), (70, 69, 70, 73),
    (70, 73, 73, 90), (73, 75, 73, 90), (75, 75, 73, 90), (76, 75, 77, 95),
    (76, 75, 78, 95), (80, 79, 83, 98), (85, 84, 85, 98), (86, 93, 86, 98),
    (91, 95, 93, 98), (94, 97, 95, 98), (98, 102, 99, 99), (101, 103, 102, 105),
    (103, 103, 105, 105), (106, 107, 106, 105), (116, 109, 108, 105), (116, 110, 108, 106),
    (116, 110, 124, 111), (118, 117, 128, 123), (124, 124, 128, 123), (130, 128, 132, 131),
    (130, 128, 132, 132), (130, 131, 132, 141), (130, 131, 133, 141), (139, 135, 140, 142),
    (143, 136, 145, 143), (148, 137, 145, 144), (151, 140, 147, 144), (153, 145, 147, 144),
    (153, 150, 147, 144), (153, 152, 155, 144), (153, 152, 158, 144), (153, 153, 158, 144),
    (161, 153, 158, 144), (161, 153, 158, 147), (161, 153, 158, 151), (166, 157, 163, 156),
    (166, 157, 165, 156), (166, 163, 169, 160), (167, 166, 171, 161), (171, 171, 171, 171),
    (171, 171, 171, 171), (171, 171, 171, 171), (171, 171, 171, 171), (171, 171, 171, 171),
]
TENSOR, SCALAR, VECTOR, GPSIMD = range(4)
T_LAG = 3
V_LAG = 5
DEPTH = 3


def schedule(engine, l0, attention):
    beats = attention_steps() if attention else []
    if not l0:
        return [("bias", i) for i in range(NB)] + [step for beat in beats for step in beat]
    out, passed = [], 0
    for step, ahead in zip(l0_steps(), BEATS_AHEAD, strict=True):
        for beat in beats[passed:ahead[engine]]:
            out += beat
        passed = ahead[engine]
        out.append(step)
    return out


def work_fills():
    fills, f = {}, 0
    for step in l0_steps():
        if step[0] in ("lin", "W", "ctx", "T", "v"):
            fills[step], f = f, f + 1
        elif step[0] == "u":
            fills[step], f = f, f + 2
    return fills, f


FILL, FILLS = work_fills()
assert FILLS % 2 == 0
BANK_FILLS = FILLS // 2


SPLIT_AHEAD = [("lin", 0, 2), ("W", 0, LEFT, 0), ("u", 0, 0), ("ctx", 0, 0), ("ctx", 0, 2), ("T", 0, 0),
               ("T", 0, 2), ("lin", 1, 1)]


def need(eng, sem, count):
    if isinstance(count, int) and count <= 0:
        return
    eng.wait_ge(sem, count)


def need_behind(eng, sem, behind, count):
    if count > 0:
        eng.wait_ge(sem, behind + count)


def stand_alone(eng, passed):
    eng.sem_inc(passed, 1)


def graph_layers(nc, x, xT, adj, adjT, wl, wr, wlinT, b_lin, ln_a, ln_b, ln_a_by_block, ln_b_by_block,
                 wq, bq_by_block, wk, bk_by_block, wv, bv, beta, out):
    with ExitStack() as ctx:
        def sb(name, shape, dt):
            return ctx.enter_context(nc.sbuf_tensor(name, shape, dt))

        def bank(name):
            return ctx.enter_context(nc.psum_tensor(name, [P, 512], F32))

        def sem(name):
            return ctx.enter_context(nc.semaphore(name))

        w_hi = sb("w_hi", [P, 9, KB, FEAT], F16)
        w_lo = sb("w_lo", [P, 9, KB, FEAT], F16)
        ident = sb("ident", [P, P], F32)
        b_lin_rows = sb("b_lin_rows", [P, LAYERS, FEAT], F32)
        ln_a_rows = sb("ln_a_rows", [P, FEAT], F32)
        ln_b_rows = sb("ln_b_rows", [P, FEAT], F32)
        bv_rows = sb("bv_rows", [P, FEAT], F32)
        ln_a_col = sb("ln_a_col", [P, KB], F32)
        ln_b_col = sb("ln_b_col", [P, KB], F32)
        qk_bias = sb("qk_bias", [P, 2, KB], F32)
        beta_col = sb("beta_col", [P, 1], F32)
        half = sb("half", [P, NB], F32)
        minus_half = sb("minus_half", [P, NB], F32)
        norm_eps = sb("norm_eps", [P, NB], F32)
        x_nodes = sb("x_nodes", [P, NB, FEAT], F32)
        hT = sb("hT", [P, KB, NODES], F32)
        xa_hi = sb("xa_hi", [P, KB, NODES], F16)
        xa_lo = sb("xa_lo", [P, KB, NODES], F16)
        xb_hi = sb("xb_hi", [P, KB, NODES], F16)
        xb_lo = sb("xb_lo", [P, KB, NODES], F16)
        hw_hi = sb("hw_hi", [P, 2, KB, NODES], F16)
        hw_lo = sb("hw_lo", [P, 2, KB, NODES], F16)
        nat = sb("nat", [P, NB, FEAT + 2], F32)
        hl_hi = sb("hl_hi", [P, NB, FEAT + 2], F32R)
        hl_lo = sb("hl_lo", [P, NB, FEAT], F32R)
        adjT_sb = sb("adjT_sb", [P, NB, NODES], F32)
        edge = sb("edge", [P, NB, NODES], F32)
        edge_diag = sb("edge_diag", [P, NB, P], F32)
        diag_part = sb("diag_part", [P, P], F32)
        erow = sb("erow", [P, 3, NODES], F32)
        e_hi = sb("e_hi", [P, NB, NODES], F32R)
        e_lo = sb("e_lo", [P, NB, NODES], F32R)
        stats = sb("stats", [P, NB, 6], F32)
        moments = sb("moments", [P, NB, 2], F32)
        var_floor = sb("var_floor", [P, NB], F32)
        deviation = sb("deviation", [P, NB], F32)
        eps_sum = sb("eps_sum", [P, NB], F32)
        denom = sb("denom", [P, NB], F32)
        factor = sb("factor", [P, NB], F32)
        shift = sb("shift", [P, NB], F32)
        stats2 = sb("stats2", [P, NB, 6], F32)
        moments2 = sb("moments2", [P, NB, 2], F32)
        var2 = sb("var2", [P, NB], F32)
        factor2 = sb("factor2", [P, NB], F32)
        shift2 = sb("shift2", [P, NB], F32)
        q_stack = sb("q_stack", [P, HEADS, NODES], F16)
        k_stack = sb("k_stack", [P, HEADS, NODES], F16)
        v_sb = sb("v_sb", [P, NB, HEADS, 2 * HD], F16)
        x2_bv = sb("x2_bv", [P, NB, FEAT], F32)
        bias = sb("bias", [P, NB, NODES], F32)
        neg_scores = sb("neg_scores", [P, 2, NODES], F32)
        masked = neg_scores[:, 0, :]
        neg_max = sb("neg_max", [P, UNITS], F32)
        probs = sb("probs", [P, DEPTH, NODES], F32)
        row_sum = sb("row_sum", [P, UNITS], F32)
        pT_hi = sb("pT_hi", [P, DEPTH, NODES], F16)
        pT_lo = sb("pT_lo", [P, DEPTH, NODES], F16)
        scaled_sum = sb("scaled_sum", [P, HEADS], F32)
        inv_sum = sb("inv_sum", [P, HEADS], F32)
        rows_out = sb("rows_out", [P, 2, FEAT], F32)
        stats3 = sb("stats3", [P, 6], F32)
        moments3 = sb("moments3", [P, 2], F32)
        var3 = sb("var3", [P, 1], F32)
        factor3 = sb("factor3", [P, 1], F32)

        work = [bank("work0"), bank("work1")]
        scores = [bank("scores0"), bank("scores1")]
        probsT = [bank("probsT0"), bank("probsT1")]
        heads_out = [bank("heads_out0"), bank("heads_out1")]

        weight_loaded = [sem(f"weight_loaded{i}") for i in range(4)]
        passed_sp, passed_dve, passed_pool = sem("passed_sp"), sem("passed_dve"), sem("passed_pool")
        weight_hi = sem("weight_hi")
        weight_lo = sem("weight_lo")
        consts_loaded = sem("consts_loaded")
        consts_scaled = sem("consts_scaled")
        pool_consts = sem("pool_consts")
        xT_loaded = sem("xT_loaded")
        x_loaded = sem("x_loaded")
        adjT_loaded = sem("adjT_loaded")
        edge_loaded = sem("edge_loaded")
        adj_loaded = sem("adj_loaded")
        selected = sem("selected")
        work_ready = sem("work_ready")
        emptied = [sem("emptied0"), sem("emptied1")]
        xa_hi_done = sem("xa_hi_done")
        xa_done = sem("xa_done")
        hi_done = sem("hi_done")
        xb_hi_done = sem("xb_hi_done")
        xb_done = sem("xb_done")
        hl_hi_done = sem("hl_hi_done")
        hl_lo_done = sem("hl_lo_done")
        z_done = sem("z_done")
        exp_done = sem("exp_done")
        e_done = sem("e_done")
        e_hi_done = sem("e_hi_done")
        e_lo_done = sem("e_lo_done")
        e_lo0_done = sem("e_lo0_done")
        stats_done = sem("stats_done")
        moments_done = sem("moments_done")
        floor_done = sem("floor_done")
        deviation_done = sem("deviation_done")
        denom_done = sem("denom_done")
        factor_done = sem("factor_done")
        shift_done = sem("shift_done")
        centered = sem("centered")
        times_a = sem("times_a")
        affine_done = sem("affine_done")
        residual_done = sem("residual_done")
        stats2_done = sem("stats2_done")
        moments2_done = sem("moments2_done")
        var2_done = sem("var2_done")
        factor2_done = sem("factor2_done")
        shift2_done = sem("shift2_done")
        normed = sem("normed")
        x2_bv_done = sem("x2_bv_done")
        masked_done = sem("masked_done")
        bias_done = sem("bias_done")
        stacked = sem("stacked")
        qk_done = sem("qk_done")
        max_done = sem("max_done")
        probs_done = sem("probs_done")
        probsT_done = sem("probsT_done")
        pT_hi_done = sem("pT_hi_done")
        pT_lo_done = sem("pT_lo_done")
        pv_done = sem("pv_done")
        reduced = sem("reduced")
        sum_scaled = sem("sum_scaled")
        sum_inverted = sem("sum_inverted")
        rows_scaled = sem("rows_scaled")
        rows_merged = sem("rows_merged")
        stats3_done = sem("stats3_done")
        moments3_done = sem("moments3_done")
        var3_done = sem("var3_done")
        factor3_done = sem("factor3_done")
        rows_done = sem("rows_done")
        stored = [sem("stored0"), sem("stored1")]

        HI_FILLS = [s for s in l0_steps() if s[0] in ("W", "v") or (s[0] == "T" and s[1] == 1)]
        HIS = len(HI_FILLS)
        STACKS = 2 * 3 * GROUP

        def fill(step):
            f = FILL[step]
            return f, f % 2, f // 2

        stage = [q_stack[:, :, :].rearrange("p a b -> p (a b)")[:, i * 2 * KB * FEAT:(i + 1) * 2 * KB * FEAT].bitcast(F32)
                 for i in (0, 1)]
        stage += [k_stack[:, :, :].rearrange("p a b -> p (a b)")[:, i * 2 * KB * FEAT:(i + 1) * 2 * KB * FEAT].bitcast(F32)
                  for i in (0, 1)]
        w_dram = [wl[0], wr[0], wlinT[0], wl[1], wr[1], wlinT[1], wq, wk, wv]
        W_ORDER = [2, 0, 1, 5, 3, 4, 6, 7, 8]

        block = ctx.enter_context(nc.Block())

        @block.sync
        def _(sp):
            def load_weight(i):
                if i >= 4:
                    sp.wait_ge(weight_lo, i - 3)
                sp.dma_start(stage[i % 4].rearrange("p (c n) -> p c n", c=KB),
                             w_dram[W_ORDER[i]].rearrange("(c p) n -> p c n", p=P)).then_inc(weight_loaded[i % 4], 16)

            def load_xT(n):
                need(sp, xb_done, KB * n)
                stand_alone(sp, passed_sp)
                sp.dma_start(hT[:, :, :], xT[bass.ds(n, 1)].rearrange("a (c p) s -> p (a c) s", p=P)).then_inc(xT_loaded, 16)

            def load_x(n):
                need(sp, residual_done, NB * n)
                stand_alone(sp, passed_sp)
                sp.dma_start(x_nodes[:, :, :], x[bass.ds(n, 1)].rearrange("a (b p) f -> p (a b) f", p=P)).then_inc(x_loaded, 16)

            def load_adj_layer0(n):
                need(sp, e_done, LAYERS * NB * n)
                stand_alone(sp, passed_sp)
                sp.dma_start(adjT_sb[:, :, :], adjT[bass.ds(n, 1)].rearrange("a (b p) s -> p (a b) s", p=P)).then_inc(adjT_loaded, 16)
                for j in range(NB):
                    rows = slice(j * P, (j + 1) * P)
                    sp.dma_start(edge[:, j, j * P:], adj[bass.ds(n, 1), rows, j * P:].rearrange("a p s -> p (a s)")).then_inc(edge_loaded, 16)
                    if j:
                        sp.dma_start(edge[:, j, 0:j * P], adjT[bass.ds(n, 1), rows, 0:j * P].rearrange("a p s -> p (a s)")).then_inc(edge_loaded, 16)

            def load_bias(n):
                need(sp, max_done, UNITS * n)
                stand_alone(sp, passed_sp)
                sp.dma_start(bias[:, :, :], adj[bass.ds(n, 1)].rearrange("a (b p) s -> p (a b) s", p=P)).then_inc(adj_loaded, 16)

            def store(a, i):
                sp.wait_ge(rows_done, a * NB + i + 1)
                stand_alone(sp, passed_sp)
                sp.dma_start(out[bass.ds(a, 1), i * P:(i + 1) * P, :].rearrange("a p f -> p (a f)"),
                             rows_out[:, i % 2, :]).then_inc(stored[i % 2], 16)

            def stack(n, side):
                f, b, q = fill(("W", 2, side, KB - 1))
                sp.wait_ge(emptied[b], n * BANK_FILLS + q + 1)
                stand_alone(sp, passed_sp)
                f, b, q = fill(("W", 2, side, KB - 2))
                sp.wait_ge(emptied[b], n * BANK_FILLS + q + 1)
                stand_alone(sp, passed_sp)
                parts = (hw_hi, hw_hi, hw_lo) if side == LEFT else (hw_hi, hw_lo, hw_hi)
                dst = q_stack if side == LEFT else k_stack
                for slot, part in enumerate(parts):
                    for g in range(GROUP):
                        sp.dma_start(dst[HD * slot:HD * (slot + 1), g:HEADS:GROUP, :],
                                     part[HD * g:HD * (g + 1), side, :, :]).then_inc(stacked, 16)

            def turn(n, l0, attention):
                a = n - 1
                if attention:
                    store(a, 0)
                if l0:
                    load_xT(n + 1)
                if attention:
                    store(a, 1)
                    store(a, 2)
                if l0:
                    load_adj_layer0(n + 1)
                    load_x(n + 1)
                if l0:
                    load_bias(n)
                    need(sp, qk_done, UNITS * n)
                    if attention:
                        stand_alone(sp, passed_sp)
                    stack(n, LEFT)
                if attention:
                    store(a, 3)
                if l0:
                    stack(n, RIGHT)

            load_xT(0)
            load_weight(0)
            load_weight(1)
            for dst, src in ((b_lin_rows[:, :, :], b_lin[:, :].partition_broadcast(P)),
                             (ln_a_rows[:, :], ln_a[1].partition_broadcast(P)),
                             (ln_b_rows[:, :], ln_b[1].partition_broadcast(P)),
                             (bv_rows[:, :], bv[:].partition_broadcast(P)),
                             (beta_col[:, :], beta[:].partition_broadcast(P)),
                             (ln_a_col[:, :], ln_a_by_block),
                             (ln_b_col[:, :], ln_b_by_block),
                             (qk_bias[:, 0, :], bq_by_block),
                             (qk_bias[:, 1, :], bk_by_block)):
                sp.dma_start(dst, src).then_inc(consts_loaded, 16)
            load_weight(2)
            load_adj_layer0(0)
            load_weight(3)
            load_x(0)
            for i in range(4, 9):
                load_weight(i)
            turn(0, True, False)
            with sp.Fori(1, GRAPHS) as n:
                turn(n, True, True)
            turn(GRAPHS, False, True)
            sp.wait_ge(xT_loaded, 16 * (GRAPHS + 1))
            sp.wait_ge(adjT_loaded, 16 * (GRAPHS + 1))
            sp.wait_ge(edge_loaded, 16 * (2 * NB - 1) * (GRAPHS + 1))
            sp.wait_ge(x_loaded, 16 * (GRAPHS + 1))
            sp.wait_ge(stored[0], 8 * NB * GRAPHS + 16)
            sp.wait_ge(stored[1], 8 * NB * GRAPHS + 16)

        @block.tensor
        def _(pe):
            def split_product(dst, lhs_hi, lhs_lo, rhs_hi, rhs_lo, ks, wait_for=None):
                for k in ks:
                    if wait_for:
                        wait_for(k)
                    for j, (a, b) in enumerate(((lhs_hi, rhs_hi), (lhs_hi, rhs_lo), (lhs_lo, rhs_hi))):
                        last = nc.tensor.matmul(dst, a(k), b(k), start=(k == ks[0] and j == 0),
                                                stop=(k == ks[-1] and j == 2))
                return last

            def bank_free(n, b, q):
                need(pe, emptied[b], n * BANK_FILLS + q)

            def emptied_all(n, step):
                f, b, q = fill(step)
                pe.wait_ge(emptied[b], n * BANK_FILLS + q + 1)
                pe.wait_ge(emptied[1 - b], n * BANK_FILLS + (f - 1) // 2 + 1)

            def layer_input(l):
                return (xa_hi, xa_lo) if l == 0 else (xb_hi, xb_lo)

            def lin(n, l, j):
                f, b, q = fill(("lin", l, j))

                def xb_split(k):
                    pe.wait_ge(xb_done, KB * n + k + 1)

                if j == 0:
                    if l == 0:
                        pe.wait_ge(xa_done, n + 1)
                        if isinstance(n, int) and n == 0:
                            pe.wait_ge(weight_lo, 1)
                    elif isinstance(n, int) and n == 0:
                        pe.wait_ge(weight_lo, 4)
                hi, lo = layer_input(l)
                bank_free(n, b, q)
                rows = slice(j * P, (j + 1) * P)
                w = 3 * l + LIN
                split_product(work[b][:, 0:FEAT], lambda k: hi[:, k, rows], lambda k: lo[:, k, rows],
                              lambda k: w_hi[:, w, k, :], lambda k: w_lo[:, w, k, :],
                              range(KB), xb_split if l and j == 0 else None).then_inc(work_ready, 1)

            def W(n, l, side, m):
                f, b, q = fill(("W", l, side, m))

                def x2_split(k):
                    _, bank, fills = fill(("T", 1, k))
                    pe.wait_ge(emptied[bank], n * BANK_FILLS + fills + 1)

                if isinstance(n, int) and n == 0 and m == 0:
                    pe.wait_ge(weight_lo, (2, 3, 5, 6, 7, 8)[2 * l + side])
                hi, lo = layer_input(l)
                bank_free(n, b, q)
                w = 3 * l + side
                cols = slice(m * P, (m + 1) * P)
                split_product(work[b][:, :], lambda k: w_hi[:, w, k, cols], lambda k: w_lo[:, w, k, cols],
                              lambda k: hi[:, k, :], lambda k: lo[:, k, :],
                              range(KB), x2_split if (l, side, m) == (2, LEFT, 0) else None).then_inc(work_ready, 1)

            def u(n, l, j):
                f, b, q = fill(("u", l, j))
                if j == 0:
                    emptied_all(n, ("W", l, LEFT, KB - 1))

                def right_split(k):
                    _, bank, fills = fill(("W", l, RIGHT, k))
                    pe.wait_ge(emptied[bank], n * BANK_FILLS + fills + 1)

                hi, lo = layer_input(l)
                rows = slice(j * P, (j + 1) * P)
                for side, cols in ((LEFT, slice(0, (j + 1) * P)), (RIGHT, slice(j * P, NODES))):
                    bb, qq = (f + side) % 2, (f + side) // 2
                    bank_free(n, bb, qq)
                    split_product(work[bb][:, cols], lambda k: hi[:, k, rows], lambda k: lo[:, k, rows],
                                  lambda k: hw_hi[:, side, k, cols], lambda k: hw_lo[:, side, k, cols],
                                  range(KB), right_split if j == 0 and side == RIGHT else None).then_inc(work_ready, 1)

            def ctx_rows(n, l, i):
                f, b, q = fill(("ctx", l, i))
                bank_free(n, b, q)
                cols = slice(i * P, (i + 1) * P)
                for j in range(NB):
                    if i == 0:
                        pe.wait_ge(hl_lo_done, (n * LAYERS + l) * NB + j + 1)
                        if j == 0:
                            pe.wait_ge(e_lo0_done, n * LAYERS + l + 1)
                        else:
                            pe.wait_ge(e_lo_done, (n * LAYERS + l) * (NB - 1) + j)
                    nc.tensor.matmul(work[b][:, 0:FEAT + 2], e_hi[:, j, cols], hl_hi[:, j, :], start=(j == 0), stop=False)
                    nc.tensor.matmul(work[b][:, 0:FEAT], e_hi[:, j, cols], hl_lo[:, j, :], start=False, stop=False)
                    last = nc.tensor.matmul(work[b][:, 0:FEAT + 2], e_lo[:, j, cols], hl_hi[:, j, :], start=False,
                                            stop=(j == NB - 1))
                last.then_inc(work_ready, 1)

            def transpose_rows(n, l, k):
                f, b, q = fill(("T", l, k))
                if k == 0:
                    if isinstance(n, int) and n == 0 and l == 0:
                        pe.wait_ge(pool_consts, 2)
                bank_free(n, b, q)
                for i in range(NB):
                    if k == 0:
                        pe.wait_ge(normed, (n * LAYERS + l) * NB + i + 1)
                    last = nc.tensor.transpose(work[b][:, i * P:(i + 1) * P], nat[:, i, k * P:(k + 1) * P], ident[:, :])
                last.then_inc(work_ready, 1)

            def v(n, j):
                f, b, q = fill(("v", j))
                if isinstance(n, int) and n == 0 and j == 0:
                    pe.wait_ge(weight_lo, 9)
                bank_free(n, b, q)
                rows = slice(j * P, (j + 1) * P)
                split_product(work[b][:, 0:FEAT], lambda k: xb_hi[:, k, rows], lambda k: xb_lo[:, k, rows],
                              lambda k: w_hi[:, W_V, k, :], lambda k: w_lo[:, W_V, k, :],
                              range(KB)).then_inc(work_ready, 1)

            def qk(a, s):
                i, h = divmod(s, HEADS)
                if s == 0:
                    pe.wait_ge(stacked, 16 * STACKS * (a + 1))
                need_behind(pe, max_done, a * UNITS, s - 1)
                nc.tensor.matmul(scores[s % 2][:, :], q_stack[0:3 * HD, h, i * P:(i + 1) * P], k_stack[0:3 * HD, h, :],
                                 start=True, stop=True).then_inc(qk_done, 1)

            def transpose_probs(a, s):
                pe.wait_ge(probs_done, a * UNITS + s + 1)
                need_behind(pe, pT_lo_done, a * UNITS, s - 1)
                for j in range(NB):
                    last = nc.tensor.transpose(probsT[s % 2][:, j * P:(j + 1) * P], probs[:, s % DEPTH, j * P:(j + 1) * P],
                                               ident[:, :])
                last.then_inc(probsT_done, 1)

            def pv(a, s):
                i, h = divmod(s, HEADS)
                b, c = divmod(h, HALF)
                pe.wait_ge(pT_lo_done, a * UNITS + s + 1)
                if s == 0:
                    pe.wait_ge(emptied[0], BANK_FILLS * (a + 1))
                    pe.wait_ge(emptied[1], BANK_FILLS * (a + 1))
                if c == 0:
                    need_behind(pe, reduced, a * 2 * NB, 2 * (i - 1) + b + 1 if i else 0)
                cols = slice(c * 2 * HD, (c + 1) * 2 * HD)
                high = slice(c * 2 * HD, c * 2 * HD + HD)
                for j in range(NB):
                    nodes = slice(j * P, (j + 1) * P)
                    nc.tensor.matmul(heads_out[b][:, cols], pT_hi[:, s % DEPTH, nodes], v_sb[:, j, h, :],
                                     start=(j == 0), stop=False)
                    last = nc.tensor.matmul(heads_out[b][:, high], pT_lo[:, s % DEPTH, nodes], v_sb[:, j, h, 0:HD],
                                            start=False, stop=(j == NB - 1))
                last.then_inc(pv_done, 1)

            def turn(n, l0, attention):
                a = n - 1
                for step in schedule(TENSOR, l0, attention):
                    kind, at = step[0], step[1:]
                    if kind == "lin":
                        lin(n, *at)
                    elif kind == "W":
                        W(n, *at)
                    elif kind == "u":
                        u(n, *at)
                    elif kind == "ctx":
                        ctx_rows(n, *at)
                    elif kind == "T":
                        transpose_rows(n, *at)
                    elif kind == "v":
                        v(n, *at)
                    elif kind == "qk":
                        qk(a, *at)
                    elif kind == "t":
                        transpose_probs(a, *at)
                    elif kind == "pv":
                        pv(a, *at)

            turn(0, True, False)
            with pe.Fori(1, GRAPHS) as n:
                turn(n, True, True)
            turn(GRAPHS, False, True)

        @block.scalar
        def _(act):
            def split_x(n):
                act.wait_ge(xT_loaded, 16 * (n + 1))
                nc.scalar.copy(xa_hi[:, :, :], hT[:, :, :]).then_inc(xa_hi_done, 1)

            def fill_high(n, dst, b, f, bias_=None, src=None):
                act.wait_ge(work_ready, n * FILLS + f + 1)
                src = work[b][:, :] if src is None else src
                if bias_ is None:
                    nc.scalar.copy(dst, src).then_inc(hi_done, 1)
                else:
                    nc.scalar.activation(dst, src, ACT.Identity, bias=bias_).then_inc(hi_done, 1)

            def W(n, l, side, m):
                f, b, q = fill(("W", l, side, m))
                if l == 0 and side == LEFT and m == 0:
                    need(act, stacked, 16 * STACKS * n)
                fill_high(n, hw_hi[:, side, m, :], b, f, qk_bias[:, side, m:m + 1] if l == 2 else None)

            def lin(n, l, j):
                f, b, q = fill(("lin", l, j))
                act.wait_ge(emptied[b], n * BANK_FILLS + q + 1)
                nc.scalar.copy(hl_hi[:, j, 0:FEAT], nat[:, j, 0:FEAT]).then_inc(hl_hi_done, 1)

            def exp_row(n, l, j):
                act.wait_ge(z_done, n * LAYERS * NB + l * NB + j + 1)
                nc.scalar.activation(erow[:, j % 3, :], erow[:, j % 3, :], ACT.Exp).then_inc(exp_done, 1)

            def e_high(n, l, j):
                act.wait_ge(e_done, n * LAYERS * NB + l * NB + j + 1)
                nc.scalar.copy(e_hi[:, j, :], erow[:, j % 3, :]).then_inc(e_hi_done, 1)

            def ctx_rows(n, l, i):
                f, b, q = fill(("ctx", l, i))
                act.wait_ge(work_ready, n * FILLS + f + 1)
                nc.scalar.copy(nat[:, i, :], work[b][:, 0:FEAT + 2]).then_inc(emptied[b], 1)

            def norm(n, l):
                if l == 0:
                    act.wait_ge(shift_done, n * LAYERS + 1)
                    for i in range(NB):
                        nc.scalar.activation(nat[:, i, 0:FEAT], nat[:, i, 0:FEAT], ACT.Identity, bias=shift[:, i:i + 1],
                                             scale=factor[:, i:i + 1]).then_inc(normed, 1)

            def relu(n, i):
                if i == 0:
                    act.wait_ge(shift_done, n * LAYERS + 2)
                nc.scalar.activation(nat[:, i, 0:FEAT], nat[:, i, 0:FEAT], ACT.Identity, bias=shift[:, i:i + 1],
                                     scale=factor[:, i:i + 1]).then_inc(centered, 1)

            def norm2(n):
                act.wait_ge(shift2_done, n + 1)
                for i in range(NB):
                    nc.scalar.activation(nat[:, i, 0:FEAT], nat[:, i, 0:FEAT], ACT.Identity, bias=shift2[:, i:i + 1],
                                         scale=factor2[:, i:i + 1]).then_inc(normed, 1)

            def transposed(n, l, k):
                f, b, q = fill(("T", l, k))
                if l == 0:
                    act.wait_ge(work_ready, n * FILLS + f + 1)
                    nc.scalar.activation(hT[:, k, :], work[b][:, :], ACT.Relu, bias=ln_b_col[:, k:k + 1],
                                         scale=ln_a_col[:, k:k + 1]).then_inc(emptied[b], 1)
                else:
                    fill_high(n, xb_hi[:, k, :], b, f)

            def v(n, j):
                f, b, q = fill(("v", j))
                fill_high(n, v_sb[:, j, :, 0:HD], b, f,
                          src=work[b][:, 0:FEAT].rearrange("p (h d) -> p h d", d=HD))

            def exp_scores(a, s):
                act.wait_ge(max_done, a * UNITS + s + 1)
                need_behind(act, probsT_done, a * UNITS, s - DEPTH + 1)
                nc.scalar.activation(probs[:, s % DEPTH, :], neg_scores[:, s % 2, :], ACT.Exp, bias=neg_max[:, s:s + 1],
                                     scale=-1.0, accum_out=row_sum[:, s:s + 1]).then_inc(probs_done, 1)

            def pT_high(a, s):
                act.wait_ge(probsT_done, a * UNITS + s + 1)
                need_behind(act, pv_done, a * UNITS, s - DEPTH + 1)
                nc.scalar.mul(pT_hi[:, s % DEPTH, :], probsT[s % 2][:, :], P_SCALE).then_inc(pT_hi_done, 1)

            def weight_high(i):
                act.wait_ge(weight_loaded[i % 4], 16 * (i // 4 + 1))
                nc.scalar.mul(w_hi[:, W_ORDER[i], :, :].rearrange("p c n -> p (c n)"), stage[i % 4],
                              W_SCALE).then_inc(weight_hi, 1)

            def turn(n, l0, attention):
                a = n - 1
                for step in schedule(SCALAR, l0, attention):
                    kind, at = step[0], step[1:]
                    if not attention and step in SPLIT_AHEAD:
                        weight_high(SPLIT_AHEAD.index(step) + 1)
                    if kind == "next_x":
                        split_x(n + 1)
                    elif kind == "W":
                        W(n, *at)
                    elif kind == "lin":
                        lin(n, *at)
                    elif kind == "u":
                        exp_row(n, *at)
                    elif kind == "E":
                        e_high(n, *at)
                    elif kind == "ctx":
                        ctx_rows(n, *at)
                    elif kind == "norm":
                        norm(n, *at)
                    elif kind == "relu":
                        relu(n, *at)
                    elif kind == "norm2":
                        norm2(n)
                    elif kind == "T":
                        transposed(n, *at)
                    elif kind == "v":
                        v(n, *at)
                    elif kind == "exp":
                        exp_scores(a, *at)
                    elif kind == "t":
                        pT_high(a, *at)

            split_x(0)
            weight_high(0)
            act.wait_ge(consts_scaled, 1)
            turn(0, True, False)
            with act.Fori(1, GRAPHS) as n:
                turn(n, True, True)
            turn(GRAPHS, False, True)

        @block.vector
        def _(dve):
            def make_bias(a, i):
                if i == 0:
                    dve.wait_ge(adj_loaded, 16 * (a + 1))
                need_behind(dve, bias_done, a * NB, i)
                nc.vector.tensor_scalar(masked, bias[:, i, :], 0.0, MASKED * SCORE_SCALE, ALU.is_le,
                                        ALU.mult).then_inc(masked_done, 1)
                dve.wait_ge(masked_done, a * NB + i + 1)
                nc.vector.scalar_tensor_tensor(out=bias[:, i, :], in0=bias[:, i, :], scalar=beta_col[:, 0:1],
                                               in1=masked, op0=ALU.mult, op1=ALU.add).then_inc(bias_done, 1)

            def hi_index(step):
                return HI_FILLS.index(step)

            def W(n, l, side, m):
                step = ("W", l, side, m)
                f, b, q = fill(step)
                dve.wait_ge(hi_done, n * HIS + hi_index(step) + 1)
                if l < 2:
                    nc.vector.tensor_sub(hw_lo[:, side, m, :], work[b][:, :], hw_hi[:, side, m, :]).then_inc(emptied[b], 1)
                else:
                    nc.vector.scalar_tensor_tensor(out=hw_lo[:, side, m, :], in0=work[b][:, :],
                                                   scalar=qk_bias[:, side, m:m + 1], in1=hw_hi[:, side, m, :],
                                                   op0=ALU.add, op1=ALU.subtract).then_inc(emptied[b], 1)

            def lin(n, l, j):
                f, b, q = fill(("lin", l, j))
                if l == 0 and j == 0:
                    need(dve, x2_bv_done, NB * n)
                dve.wait_ge(work_ready, n * FILLS + f + 1)
                nc.vector.scalar_tensor_tensor(out=nat[:, j, 0:FEAT], in0=work[b][:, 0:FEAT], scalar=1.0 / W_SCALE,
                                               in1=b_lin_rows[:, l, :], op0=ALU.mult, op1=ALU.add).then_inc(emptied[b], 1)

            def exponents(n, l, j):
                f = FILL[("u", l, j)]
                left, right = f % 2, (f + 1) % 2
                c = 1.0 / (W_SCALE * TEMPER)
                if l == 0 and j == 0:
                    dve.wait_ge(selected, n + 1)
                need(dve, z_done, n * LAYERS * NB + l * NB + j)
                if j == 3:
                    dve.wait_ge(e_lo0_done, n * LAYERS + l + 1)
                elif j == 0:
                    need(dve, e_lo_done, (n * LAYERS + l) * (NB - 1))
                dve.wait_ge(work_ready, n * FILLS + f + 1)
                if j:
                    nc.vector.scalar_tensor_tensor(out=erow[:, j % 3, 0:j * P], in0=work[left][:, 0:j * P], scalar=c,
                                                   in1=edge[:, j, 0:j * P], op0=ALU.mult, op1=ALU.mult)
                nc.vector.scalar_tensor_tensor(out=diag_part[:, :], in0=work[left][:, j * P:(j + 1) * P], scalar=c,
                                               in1=edge_diag[:, j, :], op0=ALU.mult, op1=ALU.mult).then_inc(emptied[left], 1)
                dve.wait_ge(work_ready, n * FILLS + f + 2)
                nc.vector.scalar_tensor_tensor(out=erow[:, j % 3, j * P:], in0=work[right][:, j * P:], scalar=c,
                                               in1=edge[:, j, j * P:], op0=ALU.mult, op1=ALU.mult).then_inc(emptied[right], 1)
                dve.wait_ge(emptied[right], n * BANK_FILLS + (f + 1) // 2 + 1)
                nc.vector.tensor_add(erow[:, j % 3, j * P:(j + 1) * P], erow[:, j % 3, j * P:(j + 1) * P],
                                     diag_part[:, :]).then_inc(z_done, 1)

            def e_low(n, l, j):
                if j == 0:
                    dve.wait_ge(e_hi_done, n * LAYERS * NB + l * NB + 1)
                    nc.vector.tensor_sub(e_lo[:, j, :], erow[:, j % 3, :], e_hi[:, j, :].bitcast(F32)).then_inc(e_lo0_done, 1)

            def ctx_rows(n, l, i):
                f, b, q = fill(("ctx", l, i))
                dve.wait_ge(emptied[b], n * BANK_FILLS + q + 1)
                nc.vector.bn_stats(stats[:, i, :], nat[:, i, 0:FEAT]).then_inc(stats_done, 1)

            def moments_of_ctx(n, l):
                per = n * LAYERS + l
                dve.wait_ge(stats_done, n * LAYERS * NB + (l + 1) * NB)
                stand_alone(dve, passed_dve)
                for i in range(NB):
                    last = nc.vector.bn_aggr(moments[:, i, :], stats[:, i, :])
                last.then_inc(moments_done, 1)
                nc.vector.tensor_scalar(eps_sum[:, :], nat[:, :, FEAT], 1e-10, 1e-3, ALU.add, ALU.mult)
                dve.wait_ge(moments_done, per + 1)
                nc.vector.tensor_scalar(var_floor[:, :], moments[:, :, 1], 1e-36, None, ALU.max).then_inc(floor_done, 1)

            def norm(n, l):
                per = n * LAYERS + l
                dve.wait_ge(deviation_done, per + 1)
                nc.vector.scalar_tensor_tensor(out=denom[:, :], in0=deviation[:, :],
                                               scalar=float(np.sqrt(FEAT / (FEAT - 1.0))), in1=eps_sum[:, :],
                                               op0=ALU.mult, op1=ALU.add).then_inc(denom_done, 1)
                dve.wait_ge(denom_done, per + 1)
                nc.vector.reciprocal(factor[:, :], denom[:, :]).then_inc(factor_done, 1)
                dve.wait_ge(factor_done, per + 1)
                nc.vector.scalar_tensor_tensor(out=shift[:, :], in0=moments[:, :, 0], scalar=-1.0, in1=factor[:, :],
                                               op0=ALU.mult, op1=ALU.mult).then_inc(shift_done, 1)

            def relu(n, i):
                if i == 0:
                    dve.wait_ge(x_loaded, 16 * (n + 1))
                dve.wait_ge(affine_done, n * NB + i + 1)
                nc.vector.scalar_tensor_tensor(out=nat[:, i, 0:FEAT], in0=nat[:, i, 0:FEAT], scalar=0.0,
                                               in1=x_nodes[:, i, :], op0=ALU.max, op1=ALU.add).then_inc(residual_done, 1)
                dve.wait_ge(residual_done, n * NB + i + 1)
                nc.vector.bn_stats(stats2[:, i, :], nat[:, i, 0:FEAT]).then_inc(stats2_done, 1)

            def moments2_of_rows(n):
                dve.wait_ge(stats2_done, (n + 1) * NB)
                stand_alone(dve, passed_dve)
                for i in range(NB):
                    last = nc.vector.bn_aggr(moments2[:, i, :], stats2[:, i, :])
                last.then_inc(moments2_done, 1)

            def norm2(n):
                dve.wait_ge(factor2_done, n + 1)
                nc.vector.scalar_tensor_tensor(out=shift2[:, :], in0=moments2[:, :, 0], scalar=-1.0, in1=factor2[:, :],
                                               op0=ALU.mult, op1=ALU.mult).then_inc(shift2_done, 1)

            def transposed(n, l, k):
                step = ("T", l, k)
                f, b, q = fill(step)
                if l == 0:
                    dve.wait_ge(emptied[b], n * BANK_FILLS + q + 1)
                    nc.vector.tensor_copy(xb_hi[:, k, :], hT[:, k, :]).then_inc(xb_hi_done, 1)
                    dve.wait_ge(xb_hi_done, n * KB + k + 1)
                    nc.vector.tensor_sub(xb_lo[:, k, :], hT[:, k, :], xb_hi[:, k, :]).then_inc(xb_done, 1)
                else:
                    dve.wait_ge(hi_done, n * HIS + hi_index(step) + 1)
                    nc.vector.tensor_sub(xb_lo[:, k, :], work[b][:, :], xb_hi[:, k, :]).then_inc(emptied[b], 1)

            def v(n, j):
                step = ("v", j)
                f, b, q = fill(step)
                dve.wait_ge(hi_done, n * HIS + hi_index(step) + 1)
                nc.vector.tensor_sub(v_sb[:, j, :, HD:2 * HD], work[b][:, 0:FEAT].rearrange("p (h d) -> p h d", d=HD),
                                     v_sb[:, j, :, 0:HD]).then_inc(emptied[b], 1)

            def masked_scores(a, s):
                i, h = divmod(s, HEADS)
                if s == 0:
                    dve.wait_ge(bias_done, NB * (a + 1))
                dve.wait_ge(qk_done, a * UNITS + s + 1)
                need_behind(dve, probs_done, a * UNITS, s - 1)
                stand_alone(dve, passed_dve)
                nc.vector.tensor_tensor_reduce(out=neg_scores[:, s % 2, :], in0=scores[s % 2][:, :], in1=bias[:, i, :],
                                               scale=-1.0 / SCORE_SCALE, scalar=3.0e38, op0=ALU.add, op1=ALU.min,
                                               accum_out=neg_max[:, s:s + 1]).then_inc(max_done, 1)

            def pT_low(a, s):
                dve.wait_ge(pT_hi_done, a * UNITS + s + 1)
                nc.vector.scalar_tensor_tensor(out=pT_lo[:, s % DEPTH, :], in0=probsT[s % 2][:, :], scalar=P_SCALE,
                                               in1=pT_hi[:, s % DEPTH, :], op0=ALU.mult, op1=ALU.subtract).then_inc(pT_lo_done, 1)

            def reduce(a, i, b):
                dve.wait_ge(pv_done, a * UNITS + HEADS * i + HALF * (b + 1))
                dve.wait_ge(stored[i % 2], 16 * (a * (NB // 2) + i // 2 + 1))
                nc.vector.tensor_reduce(
                    rows_out[:, i % 2, b * HALF * HD:(b + 1) * HALF * HD].rearrange("p (h d) -> p h d", d=HD),
                    heads_out[b][:, 0:HALF * 2 * HD].rearrange("p (h e d) -> p h d e", e=2, d=HD),
                    axis=AX.X, op=ALU.add).then_inc(reduced, 1)

            def merge(a, i):
                dve.wait_ge(probs_done, a * UNITS + HEADS * (i + 1))
                need_behind(dve, rows_scaled, a * NB, i)
                nc.vector.tensor_scalar(scaled_sum[:, :], row_sum[:, HEADS * i:HEADS * (i + 1)], W_SCALE * P_SCALE, None,
                                        ALU.mult).then_inc(sum_scaled, 1)
                dve.wait_ge(sum_scaled, a * NB + i + 1)
                nc.vector.reciprocal(inv_sum[:, :], scaled_sum[:, :]).then_inc(sum_inverted, 1)

            def moments_of_rows(a, i):
                dve.wait_ge(rows_merged, a * NB + i + 1)
                need_behind(dve, rows_done, a * NB, i)
                nc.vector.bn_stats(stats3[:, :], rows_out[:, i % 2, :]).then_inc(stats3_done, 1)
                dve.wait_ge(stats3_done, a * NB + i + 1)
                stand_alone(dve, passed_dve)
                nc.vector.bn_aggr(moments3[:, :], stats3[:, :]).then_inc(moments3_done, 1)

            def finish(a, i):
                dve.wait_ge(factor3_done, a * NB + i + 1)
                nc.vector.tensor_scalar(rows_out[:, i % 2, :], rows_out[:, i % 2, :], moments3[:, 0:1], factor3[:, 0:1],
                                        ALU.subtract, ALU.mult).then_inc(rows_done, 1)

            def weight_low(i):
                dve.wait_ge(weight_hi, i + 1)
                nc.vector.scalar_tensor_tensor(out=w_lo[:, W_ORDER[i], :, :].rearrange("p c n -> p (c n)"), in0=stage[i % 4],
                                               scalar=W_SCALE, in1=w_hi[:, W_ORDER[i], :, :].rearrange("p c n -> p (c n)"),
                                               op0=ALU.mult, op1=ALU.subtract).then_inc(weight_lo, 1)

            def turn(n, l0, attention):
                a = n - 1
                for step in schedule(VECTOR, l0, attention):
                    kind, at = step[0], step[1:]
                    if not attention and step in SPLIT_AHEAD:
                        weight_low(SPLIT_AHEAD.index(step) + 1)
                    if kind == "W":
                        W(n, *at)
                    elif kind == "lin":
                        lin(n, *at)
                    elif kind == "u":
                        exponents(n, *at)
                    elif kind == "E":
                        e_low(n, *at)
                    elif kind == "ctx":
                        ctx_rows(n, *at)
                    elif kind == "moments0":
                        moments_of_ctx(n, *at)
                    elif kind == "norm":
                        norm(n, *at)
                    elif kind == "relu":
                        relu(n, *at)
                    elif kind == "moments2":
                        moments2_of_rows(n)
                    elif kind == "norm2":
                        norm2(n)
                    elif kind == "T":
                        transposed(n, *at)
                    elif kind == "bias" and attention:
                        make_bias(a, *at)
                    elif kind == "v":
                        v(n, *at)
                    elif kind == "qk":
                        masked_scores(a, *at)
                    elif kind == "low_t":
                        pT_low(a, *at)
                    elif kind == "reduce":
                        reduce(a, *at)
                    elif kind == "merge":
                        merge(a, *at)
                    elif kind == "moments":
                        moments_of_rows(a, *at)
                    elif kind == "finish":
                        finish(a, *at)

            nc.vector.memset(hl_hi[:, :, FEAT:FEAT + 2].bitcast(F32), 1.0)
            dve.sem_inc(stored[0], 16)
            dve.sem_inc(stored[1], 16)
            dve.wait_ge(xa_hi_done, 1)
            nc.vector.tensor_sub(xa_lo[:, :, :], hT[:, :, :], xa_hi[:, :, :]).then_inc(xa_done, 1)
            weight_low(0)
            dve.wait_ge(consts_loaded, 16 * 9)
            nc.vector.tensor_scalar(beta_col[:, :], beta_col[:, :], SCORE_SCALE, None, ALU.mult)
            nc.vector.tensor_scalar(qk_bias[:, :, :], qk_bias[:, :, :], W_SCALE, None, ALU.mult).then_inc(consts_scaled, 1)
            dve.wait_ge(consts_scaled, 1)
            turn(0, True, False)
            with dve.Fori(1, GRAPHS) as n:
                turn(n, True, True)
            turn(GRAPHS, False, True)

        @block.gpsimd
        def _(pool):
            def split_x(n):
                pool.wait_ge(xa_hi_done, n + 1)
                nc.gpsimd.tensor_sub(xa_lo[:, :, :], hT[:, :, :], xa_hi[:, :, :]).then_inc(xa_done, 1)

            def select(n):
                pool.wait_ge(adjT_loaded, 16 * (n + 1))
                pool.wait_ge(edge_loaded, 16 * (2 * NB - 1) * (n + 1))
                stand_alone(pool, passed_pool)
                for j in range(NB):
                    cols = slice(j * P, (j + 1) * P)
                    nc.gpsimd.affine_select(out=edge_diag[:, j, :], in_=adjT_sb[:, j, cols], compare_op=ALU.is_ge,
                                            fill=0.0, base=0, pattern=[[-1, P]], channel_multiplier=1)
                    last = nc.gpsimd.affine_select(out=edge[:, j, cols], in_=edge[:, j, cols], compare_op=ALU.is_gt,
                                                   fill=0.0, base=0, pattern=[[1, P]], channel_multiplier=-1)
                last.then_inc(selected, 1)

            def e_low(n, l, j):
                if j == 0:
                    return
                pool.wait_ge(e_hi_done, n * LAYERS * NB + l * NB + j + 1)
                nc.gpsimd.tensor_sub(e_lo[:, j, :], erow[:, j % 3, :], e_hi[:, j, :].bitcast(F32)).then_inc(e_lo_done, 1)

            def hl_low(n, l, j):
                pool.wait_ge(hl_hi_done, n * LAYERS * NB + l * NB + j + 1)
                nc.gpsimd.tensor_sub(hl_lo[:, j, :], nat[:, j, 0:FEAT], hl_hi[:, j, 0:FEAT].bitcast(F32)).then_inc(hl_lo_done, 1)

            def times_adj(n, l, j):
                pool.wait_ge(exp_done, n * LAYERS * NB + l * NB + j + 1)
                nc.gpsimd.tensor_mul(erow[:, j % 3, :], erow[:, j % 3, :], adjT_sb[:, j, :]).then_inc(e_done, 1)

            def deviation_of_ctx(n, l):
                pool.wait_ge(floor_done, n * LAYERS + l + 1)
                nc.gpsimd.tensor_tensor(deviation[:, :], var_floor[:, :], half[:, :], ALU.pow).then_inc(deviation_done, 1)

            def relu(n, i):
                pool.wait_ge(centered, n * NB + i + 1)
                nc.gpsimd.tensor_mul(nat[:, i, 0:FEAT], nat[:, i, 0:FEAT], ln_a_rows[:, :]).then_inc(times_a, 1)
                pool.wait_ge(times_a, n * NB + i + 1)
                nc.gpsimd.tensor_add(nat[:, i, 0:FEAT], nat[:, i, 0:FEAT], ln_b_rows[:, :]).then_inc(affine_done, 1)

            def factor_of_x2(n):
                pool.wait_ge(moments2_done, n + 1)
                nc.gpsimd.tensor_add(var2[:, :], moments2[:, :, 1], norm_eps[:, :]).then_inc(var2_done, 1)
                pool.wait_ge(var2_done, n + 1)
                nc.gpsimd.tensor_tensor(factor2[:, :], var2[:, :], minus_half[:, :], ALU.pow).then_inc(factor2_done, 1)

            def residual(n):
                pool.wait_ge(normed, n * LAYERS * NB + 2 * NB)
                for i in range(NB):
                    nc.gpsimd.tensor_add(x2_bv[:, i, :], nat[:, i, 0:FEAT], bv_rows[:, :]).then_inc(x2_bv_done, 1)

            def merge(a, i):
                pool.wait_ge(sum_inverted, a * NB + i + 1)
                pool.wait_ge(reduced, a * 2 * NB + 2 * i + 2)
                rows = rows_out[:, i % 2, :].rearrange("p (h d) -> p h d", d=HD)
                nc.gpsimd.tensor_tensor(rows, rows, inv_sum[:, :].unsqueeze(2).to_broadcast([P, HEADS, HD]),
                                        ALU.mult).then_inc(rows_scaled, 1)
                pool.wait_ge(rows_scaled, a * NB + i + 1)
                nc.gpsimd.tensor_add(rows_out[:, i % 2, :], rows_out[:, i % 2, :], x2_bv[:, i, :]).then_inc(rows_merged, 1)

            def factor_of_rows(a, i):
                pool.wait_ge(moments3_done, a * NB + i + 1)
                nc.gpsimd.tensor_add(var3[:, :], moments3[:, 1:2], norm_eps[:, 0:1]).then_inc(var3_done, 1)
                pool.wait_ge(var3_done, a * NB + i + 1)
                nc.gpsimd.tensor_tensor(factor3[:, :], var3[:, :], minus_half[:, 0:1], ALU.pow).then_inc(factor3_done, 1)

            def turn(n, l0, attention):
                a = n - 1
                for step in schedule(GPSIMD, l0, attention):
                    kind, at = step[0], step[1:]
                    if kind == "next_x":
                        split_x(n + 1)
                        select(n + 1)
                    elif kind == "E":
                        e_low(n, *at)
                    elif kind == "residual":
                        residual(n)
                    elif kind == "lin":
                        hl_low(n, *at)
                    elif kind == "u":
                        times_adj(n, *at)
                    elif kind == "moments0":
                        deviation_of_ctx(n, *at)
                    elif kind == "relu":
                        relu(n, *at)
                    elif kind == "moments2":
                        factor_of_x2(n)
                    elif kind == "merge":
                        merge(a, *at)
                    elif kind == "moments":
                        factor_of_rows(a, *at)

            nc.gpsimd.memset(half[:, :], 0.5)
            nc.gpsimd.memset(minus_half[:, :], -0.5)
            nc.gpsimd.memset(norm_eps[:, :], 1e-5)
            nc.gpsimd.memset(ident[:, :], 0.0).then_inc(pool_consts, 1)
            pool.wait_ge(pool_consts, 1)
            nc.gpsimd.affine_select(out=ident[:, :], in_=ident[:, :], compare_op=ALU.not_equal, fill=1.0, base=0,
                                    pattern=[[-1, P]], channel_multiplier=1).then_inc(pool_consts, 1)
            select(0)
            turn(0, True, False)
            with pool.Fori(1, GRAPHS) as n:
                turn(n, True, True)
            turn(GRAPHS, False, True)


def kernel(**inputs):
    import concourse.bacc as bacc
    from concourse.bass_utils import run_bass_kernel_spmd

    def one_more(a):
        return np.concatenate([a, a[:1]])

    def by_block(a):
        return np.asarray(a).reshape(KB, P).T

    x = np.asarray(inputs["x"])
    adj = np.asarray(inputs["adj"])
    arrays = {
        "x": one_more(x),
        "xT": one_more(x.transpose(0, 2, 1)),
        "adj": one_more(adj),
        "adjT": one_more(adj.transpose(0, 2, 1)),
        "wl": inputs["L0_gnn_W_left"],
        "wr": inputs["L0_gnn_W_right"],
        "wlinT": np.asarray(inputs["L0_gnn_W_lin"]).transpose(0, 2, 1),
        "b_lin": inputs["L0_gnn_b_lin"],
        "ln_a": inputs["L0_gnn_ln_a"],
        "ln_b": inputs["L0_gnn_ln_b"],
        "ln_a_by_block": by_block(inputs["L0_gnn_ln_a"][0]),
        "ln_b_by_block": by_block(inputs["L0_gnn_ln_b"][0]),
        "wq": inputs["L1_gnn_Wq"],
        "bq_by_block": by_block(inputs["L1_gnn_bq"]),
        "wk": inputs["L1_gnn_Wk"],
        "bk_by_block": by_block(inputs["L1_gnn_bk"]),
        "wv": inputs["L1_gnn_Wv"],
        "bv": inputs["L1_gnn_bv"],
        "beta": np.asarray(inputs["L1_gnn_beta"]).reshape(1),
    }
    arrays = {f"in_{k}": np.ascontiguousarray(v) for k, v in arrays.items()}
    nc = bacc.Bacc("TRN2", target_bir_lowering=False, num_devices=1)
    args = [nc.dram_tensor(k, v.shape, mybir.dt.from_np(v.dtype), kind="ExternalInput").ap() for k, v in arrays.items()]
    out = nc.dram_tensor("out_0", (GRAPHS, NODES, FEAT), F32, kind="ExternalOutput").ap()
    graph_layers(nc, *args, out)
    r = run_bass_kernel_spmd(nc, [arrays], core_ids=[0])
    return r.results[0]["out_0"]
```
